# Optimizing a Trainium2 kernel written in Bass

```python
import numpy as np
import jax
import jax.numpy as jnp

def _softmax(x, axis=-1):
    return jax.nn.softmax(x, axis=axis)

def _gelu(x):
    return jax.nn.gelu(x, approximate=True)

def _silu(x):
    return jax.nn.silu(x)

def _sigmoid(x):
    return jax.nn.sigmoid(x)

def _layernorm(x, axis=-1, eps=1e-05):
    m = jnp.mean(x, axis=axis, keepdims=True)
    v = jnp.var(x, axis=axis, keepdims=True)
    return (x - m) / jnp.sqrt(v + eps)

def _scatter_add(tgt, idx, src, axis=0):
    return tgt.at[idx].add(src)

def _segment_sum(src, seg, n):
    return jax.ops.segment_sum(src, seg, n)
kernel_name = 'mk_seq_postln_d1_jaxref_r8_c7dcdc'

def setup_inputs(seed: int=0):
    np.random.seed(seed)
    _w = jnp.asarray

    def _L0_attn_setup():
        import jax, jax.numpy as jnp
        import numpy as np
        D_INNER, D_STATE, DT_RANK = (256, 16, 128)
        BATCH, SEQ = (2, 256)

        def _selective_scan(u, delta, A, B, C, D):
            dA = jnp.exp(delta[..., None] * A[None, None])
            dBu = (delta * u)[..., None] * B[:, :, None, :]

            def step(h, inp):
                dA_t, dBu_t, C_t = inp
                h = dA_t * h + dBu_t
                y_t = jnp.einsum('bdn,bn->bd', h, C_t)
                return (h, y_t)
            h0 = jnp.zeros((u.shape[0], u.shape[2], A.shape[1]), dtype=u.dtype)
            xs = (jnp.moveaxis(dA, 1, 0), jnp.moveaxis(dBu, 1, 0), jnp.moveaxis(C, 1, 0))
            _, ys = jax.lax.scan(step, h0, xs)
            y = jnp.moveaxis(ys, 0, 1)
            return y + u * D[None, None, :]
        key = jax.random.key(seed)
        ks = jax.random.split(key, 6)
        x = jax.random.normal(ks[0], (BATCH, SEQ, D_INNER), dtype=jnp.float32)
        A_log = jax.random.uniform(ks[1], (D_INNER, D_STATE), minval=-4.0, maxval=-1.0, dtype=jnp.float32)
        D = jnp.ones((D_INNER,), dtype=jnp.float32)
        x_proj_w = jax.random.normal(ks[2], (DT_RANK + 2 * D_STATE, D_INNER), dtype=jnp.float32) / np.sqrt(D_INNER)
        dt_proj_w = jax.random.normal(ks[3], (D_INNER, DT_RANK), dtype=jnp.float32) / np.sqrt(DT_RANK)
        dt_std = DT_RANK ** (-0.5)
        dt_proj_b = jax.random.uniform(ks[4], (D_INNER,), minval=-dt_std, maxval=dt_std, dtype=jnp.float32)
        return {'x': x, 'A_log': A_log, 'D': D, 'x_proj_w': x_proj_w, 'dt_proj_w': dt_proj_w, 'dt_proj_b': dt_proj_b}
    _L0_attn_in = _L0_attn_setup()

    def _L0_ffn_setup():
        import jax, jax.numpy as jnp
        import numpy as np
        from jax import lax
        E = 8
        K = 2
        H = 256
        I = 512
        B, S = (2, 256)
        SCALE = 0.02

        def _silu_and_mul(gu):
            g, u = jnp.split(gu, 2, axis=-1)
            return jax.nn.silu(g) * u
        key = jax.random.key(seed)
        ks = jax.random.split(key, 6)
        return {'hidden_states': jax.random.normal(ks[0], (B, S, H), dtype=jnp.float32), 'gate_w': jax.random.normal(ks[1], (H, E), dtype=jnp.float32) * SCALE, 'w_gate_up': jax.random.normal(ks[2], (E, H, 2 * I), dtype=jnp.float32) * SCALE, 'w_down': jax.random.normal(ks[3], (E, I, H), dtype=jnp.float32) * SCALE, 'shared_gate_up': jax.random.normal(ks[4], (H, 2 * I), dtype=jnp.float32) * SCALE, 'shared_down': jax.random.normal(ks[5], (I, H), dtype=jnp.float32) * SCALE}
    _L0_ffn_in = _L0_ffn_setup()
    _d = {'L0_attn_x': _L0_attn_in['x'], 'L0_attn_A_log': _L0_attn_in['A_log'], 'L0_attn_D': _L0_attn_in['D'], 'L0_attn_x_proj_w': _L0_attn_in['x_proj_w'], 'L0_attn_dt_proj_w': _L0_attn_in['dt_proj_w'], 'L0_attn_dt_proj_b': _L0_attn_in['dt_proj_b'], 'L0_ffn_gate_w': _L0_ffn_in['gate_w'], 'L0_ffn_w_gate_up': _L0_ffn_in['w_gate_up'], 'L0_ffn_w_down': _L0_ffn_in['w_down'], 'L0_ffn_shared_gate_up': _L0_ffn_in['shared_gate_up'], 'L0_ffn_shared_down': _L0_ffn_in['shared_down']}
    _x0 = _d['L0_attn_x']
    _d['L0_attn_x'] = jax.random.normal(jax.random.fold_in(jax.random.key(seed), 1), (4, 512, 256), dtype=_x0.dtype)
    del _x0
    return _d

def reference(L0_attn_x, L0_attn_A_log, L0_attn_D, L0_attn_x_proj_w, L0_attn_dt_proj_w, L0_attn_dt_proj_b, L0_ffn_gate_w, L0_ffn_w_gate_up, L0_ffn_w_down, L0_ffn_shared_gate_up, L0_ffn_shared_down):

    def _L0_attn_ref(x, A_log, D, x_proj_w, dt_proj_w, dt_proj_b):
        import jax, jax.numpy as jnp
        import numpy as np
        D_INNER, D_STATE, DT_RANK = (256, 16, 128)
        BATCH, SEQ = (2, 256)

        def _selective_scan(u, delta, A, B, C, D):
            dA = jnp.exp(delta[..., None] * A[None, None])
            dBu = (delta * u)[..., None] * B[:, :, None, :]

            def step(h, inp):
                dA_t, dBu_t, C_t = inp
                h = dA_t * h + dBu_t
                y_t = jnp.einsum('bdn,bn->bd', h, C_t)
                return (h, y_t)
            h0 = jnp.zeros((u.shape[0], u.shape[2], A.shape[1]), dtype=u.dtype)
            xs = (jnp.moveaxis(dA, 1, 0), jnp.moveaxis(dBu, 1, 0), jnp.moveaxis(C, 1, 0))
            _, ys = jax.lax.scan(step, h0, xs)
            y = jnp.moveaxis(ys, 0, 1)
            return y + u * D[None, None, :]
        x_dbl = jnp.einsum('bld,ed->ble', x, x_proj_w)
        delta_r = x_dbl[..., :DT_RANK]
        B = x_dbl[..., DT_RANK:DT_RANK + D_STATE]
        C = x_dbl[..., DT_RANK + D_STATE:]
        delta = jnp.einsum('blr,dr->bld', delta_r, dt_proj_w) + dt_proj_b
        delta = jax.nn.softplus(delta)
        A = -jnp.exp(A_log)
        return _selective_scan(x, delta, A, B, C, D)

    def _L0_ffn_ref(hidden_states, gate_w, w_gate_up, w_down, shared_gate_up, shared_down):
        import jax, jax.numpy as jnp
        import numpy as np
        from jax import lax
        E = 8
        K = 2
        H = 256
        I = 512
        B, S = (2, 256)
        SCALE = 0.02

        def _silu_and_mul(gu):
            g, u = jnp.split(gu, 2, axis=-1)
            return jax.nn.silu(g) * u
        orig_shape = hidden_states.shape
        x = hidden_states.reshape(-1, orig_shape[-1])
        shared_out = _silu_and_mul(x @ shared_gate_up) @ shared_down
        router_logits = x @ gate_w
        probs = jax.nn.softmax(router_logits, axis=-1)
        topk_w, topk_i = lax.top_k(probs, K)
        topk_w = topk_w / jnp.sum(topk_w, axis=-1, keepdims=True)
        combine = jnp.sum(jax.nn.one_hot(topk_i, E, dtype=x.dtype) * topk_w[..., None], axis=1)

        def body(acc, we):
            wg, wd, cw = we
            h = _silu_and_mul(x @ wg) @ wd
            return (acc + cw[:, None] * h, None)
        moe_out, _ = lax.scan(body, jnp.zeros_like(x), (w_gate_up, w_down, combine.T))
        return (moe_out + shared_out).reshape(orig_shape)
    x = L0_attn_x
    x = _layernorm(x + _L0_attn_ref(x, L0_attn_A_log, L0_attn_D, L0_attn_x_proj_w, L0_attn_dt_proj_w, L0_attn_dt_proj_b), axis=-1)
    x = _layernorm(x + _L0_ffn_ref(x, L0_ffn_gate_w, L0_ffn_w_gate_up, L0_ffn_w_down, L0_ffn_shared_gate_up, L0_ffn_shared_down), axis=-1)
    return x

_drawn_inputs = setup_inputs


def setup_inputs(seed=0):
    import zlib

    import numpy as np

    out = dict(_drawn_inputs(seed))
    spreads = {'L0_attn_D': (1.0, 0.6)}
    factors = {'L0_attn_dt_proj_b': 2.868,
     'L0_ffn_gate_w': 3.872,
     'L0_ffn_w_gate_up': 3.332,
     'L0_ffn_w_down': 3.335,
     'L0_ffn_shared_gate_up': 3.002,
     'L0_ffn_shared_down': 3.005}
    for name, (base, spread) in spreads.items():
        noise = np.random.default_rng([zlib.crc32(name.encode()), seed]).standard_normal(out[name].shape)
        drawn = base * np.exp(spread * noise) if base else spread * noise
        out[name] = jnp.asarray(drawn.astype(out[name].dtype))
    for name, factor in factors.items():
        out[name] = (out[name] * factor).astype(out[name].dtype)
    return out
```

```python
from contextlib import ExitStack

import concourse.bass as bass
from concourse import mybir

ALU = mybir.AluOpType
ACT = mybir.ActivationFunctionType
F32 = mybir.dt.float32
BF16 = mybir.dt.bfloat16
I32 = mybir.dt.int32
U32 = mybir.dt.uint32
AX = mybir.AxisListType
ds = bass.ds

P = 128
EPS = 1e-5


class Chain:

    def __init__(self, engine, sem):
        self.engine, self.sem, self.base, self.n = engine, sem, 0, 0

    def link(self, instruction, alone=None):
        self.n += 1
        instruction.then_inc(self.sem, 1)
        self.engine.wait_ge(self.sem, self.base + self.n)
        if alone:
            alone(self.engine)

    def start(self, base):
        self.base, self.n = base, 0


def mamba_moe(nc, x, a_log, d_skip, x_proj_w, dt_w, dt_b, gate_w, w_gu, w_dn, ws_gu, ws_dn, out):
    NB, L, D = x.shape
    N = a_log.shape[1]
    R = dt_w.shape[1]
    E, _, F2 = w_gu.shape
    F = F2 // 2
    H = D // P
    NT = NB * L // P
    TB = L // P
    KF = F // P
    TOP = 2
    BC = 2 * N
    PARTS = 3
    RT = (NT * P * TOP + E * (P - 1)) // P
    RT += RT % 2
    REGION = NT * P + P
    SPARE = RT - NT * TOP
    ROWS = E * REGION + SPARE * P
    assert H == 2 and R == P and L == 512 and F == 512 and E == 8 and N == 16

    slots = nc.dram_tensor("slots_x", (ROWS, D), F32, kind="Internal").ap()
    slots_y = nc.dram_tensor("slots_y", (RT * P, D), F32, kind="Internal").ap()
    x_view = x.rearrange("b (j p) d -> p (b j) d", p=P)
    out_view = out.rearrange("b (j p) d -> p (b j) d", p=P)

    with ExitStack() as ctx:
        def sb(name, shape, dt=F32):
            return ctx.enter_context(nc.sbuf_tensor(name, shape, dt))

        def sem(name):
            return ctx.enter_context(nc.semaphore(name))

        wgu = sb("wgu", [P, (E + 1) * H * F2])
        wds = sb("wds", [P, KF * D])
        x1 = sb("x1", [P, NT, D])
        xT = sb("xT", [P, H, NB * L])
        stack = sb("stack", [PARTS * BC, NB * L], BF16)
        sel = sb("sel", [PARTS * BC, BC, P], BF16)
        vb = sb("vb", [P, H, L])
        ident = sb("ident", [P, P])
        tri = sb("tri", [P, P], BF16)
        ones = sb("ones", [P, P], BF16)
        zeros = sb("zeros", [P, D])
        wT = sb("wT", [P, 4 * P])
        wbcT = sb("wbcT", [P, H, PARTS * BC])
        alog = sb("alog", [P, H, N])
        aexp = sb("aexp", [P, H, N])
        aneg = sb("aneg", [P, H, N])
        dsk = sb("dsk", [P, H])
        dsk1 = sb("dsk1", [P, H])
        dtb = sb("dtb", [P, H])
        gw = sb("gw", [P, H, E])
        st6 = sb("st6", [P, TB, 6])
        mv = sb("mv", [P, TB, 2])
        ve = sb("ve", [P, TB])
        lnv = sb("lnv", [P, TB])
        r0 = sb("r0", [P, TB])
        r1 = sb("r1", [P, TB])
        r2 = sb("r2", [P, TB])
        r3 = sb("r3", [P, TB])
        rstd = sb("rstd", [P, TB])
        iota8 = sb("iota8", [P, E])
        base8 = sb("base8", [P, E])
        lg = sb("lg", [P, E])
        mx8 = sb("mx8", [P, 8])
        ix8 = sb("ix8", [P, 8], U32)
        ixf = sb("ixf", [P, TOP])
        oh = sb("oh", [P, 2, TOP, E])
        mask = sb("mask", [P, 2, E], BF16)
        cum = sb("cum", [P, 2, E], BF16)
        rank8 = sb("rank8", [P, E])
        pick = sb("pick", [P, TOP, E])
        slotf = sb("slotf", [P, TOP])
        idx_all = sb("idx_all", [P, NT * TOP], U32)
        idx_now = sb("idx_now", [P, 2, TOP], U32)
        slot_all = sb("slot_all", [P, NT * TOP])
        ex_all = sb("ex_all", [P, NT * TOP])
        starts = sb("starts", [P, E])
        shift = sb("shift", [P, E])
        back = sb("back", [P, NT * TOP])
        row_y = sb("row_y", [P, NT * TOP])
        dif = sb("dif", [P, NT])
        edif = sb("edif", [P, NT])
        eden = sb("eden", [P, NT])
        wt0 = sb("wt0", [P, NT])
        wt1 = sb("wt1", [P, NT])
        cnt = sb("cnt", [P, E])
        cnti = sb("cnti", [P, E], I32)
        pgi = sb("pgi", [P, E], I32)
        pgs = sb("pgs", [P, E], I32)
        pages = sb("pages", [P, E])
        onerow = sb("onerow", [P, E])
        ends = sb("ends", [P, E])
        skip = sb("skip", [P, E])
        jrow = sb("jrow", [1, RT])
        jbase = sb("jbase", [1, RT])
        esum = sb("esum", [1, RT])
        rsum = sb("rsum", [1, RT])
        rowf = sb("rowf", [1, RT])
        tab_e = sb("tab_e", [1, RT], I32)
        tab_r = sb("tab_r", [1, RT], I32)

        RING = 4
        arena = sb("arena", [P, 18432])
        at = [0]

        def room(n):
            at[0] += n
            assert at[0] <= 18432
            return arena[:, at[0] - n:at[0]]

        dA = room(2 * H * L).rearrange("p (s h l) -> p s h l", s=2, h=H)
        dBu = room(RING * H * L).rearrange("p (s h l) -> p s h l", s=RING, h=H)
        h_at = at[0]
        hs = room(2 * H * L).rearrange("p (s h l) -> p s h l", s=2, h=H)
        hC = room(2 * H * L).rearrange("p (s h l) -> p s h l", s=2, h=H)
        delta = room(H * NB * L).rearrange("p (h l) -> p h l", h=H)
        du = room(H * NB * L).rearrange("p (h l) -> p h l", h=H)
        at[0] = 0
        wx = room(D)
        wbc = room(D)[0:PARTS * BC, :]
        dtw = room(H * R).rearrange("p (h r) -> p h r", h=H)
        at[0] = h_at
        xs = room(TB * D).rearrange("p (j d) -> p j d", j=TB)
        drT = room(L)
        ab = room(H * L).rearrange("p (h l) -> p h l", h=H)
        zb = room(H * L).rearrange("p (h l) -> p h l", h=H)
        at[0] = 0
        wdn = room(E * KF * D)
        x1s = room(2 * D).rearrange("p (s d) -> p s d", s=2)
        xsc = room(2 * D).rearrange("p (s d) -> p s d", s=2)
        xTs = room(2 * D).rearrange("p (s k m) -> p s k m", s=2, k=H)
        gs = room(F)
        hp = room(F)
        hT = room(F).rearrange("p (k m) -> p k m", k=KF)
        yo = room(2 * D).rearrange("p (s d) -> p s d", s=2)
        gat = room(TB * TOP * D).rearrange("p (j k d) -> p j k d", j=TB, k=TOP)
        vfin = room(TB * D).rearrange("p (j d) -> p j d", j=TB)
        ofin = room(TB * D).rearrange("p (j d) -> p j d", j=TB)
        is_ex = room(NT * TOP * E).rearrange("p (t e) -> p t e", e=E)
        moved = room(NT * TOP * E).rearrange("p (t e) -> p t e", e=E)
        past = room(RT * E)[0:1, :].rearrange("p (t e) -> p t e", e=E)
        jump = room(RT * E)[0:1, :].rearrange("p (t e) -> p t e", e=E)

        bank = [ctx.enter_context(nc.psum_tensor(f"bank{i}", [P, 512], F32)) for i in range(8)]
        psB, psC, psY = bank[0:2], bank[2:4], bank[4:6]
        psV = bank[6:8]
        psG, psU, psX, psH, psO, psL, psR, psN = bank

        small_in = sem("small_in")
        x_in = sem("x_in")
        shared_in = sem("shared_in")
        gu_in = sem("gu_in")
        dn_in = sem("dn_in")
        consts = sem("consts")
        pool_steps = sem("pool_steps")
        wT_made = sem("wT_made")
        wT_ready = sem("wT_ready")
        a_exp = sem("a_exp")
        a_ready = sem("a_ready")
        x_turned = sem("x_turned")
        xT_act = sem("xT_act")
        xT_dve = sem("xT_dve")
        dr_made = sem("dr_made")
        bc_made = sem("bc_made")
        dr_kept = sem("dr_kept")
        bc_read = sem("bc_read")
        z_made = sem("z_made")
        zb_ready = sem("zb_ready")
        ab_ready = sem("ab_ready")
        prep_done = sem("prep_done")
        v_steps = sem("v_steps")
        s_steps = sem("s_steps")
        B_ready = sem("B_ready")
        C_ready = sem("C_ready")
        dBu_ready = sem("dBu_ready")
        dA_ready = sem("dA_ready")
        h_ready = sem("h_ready")
        hC_ready = sem("hC_ready")
        y_added = sem("y_added")
        v_ready = sem("v_ready")
        v_turned = sem("v_turned")
        var_ready = sem("var_ready")
        rstd_ready = sem("rstd_ready")
        x1_ready = sem("x1_ready")
        x1_copied = sem("x1_copied")
        X_turned = sem("X_turned")
        XT_ready = sem("XT_ready")
        L_made = sem("L_made")
        G_made = sem("G_made")
        U_made = sem("U_made")
        silu_done = sem("silu_done")
        hp_ready = sem("hp_ready")
        H_turned = sem("H_turned")
        hT_ready = sem("hT_ready")
        O_made = sem("O_made")
        O_read = sem("O_read")
        L_read = sem("L_read")
        mask_ready = sem("mask_ready")
        rank_made = sem("rank_made")
        idx_ready = sem("idx_ready")
        scattered = [sem("scattered0"), sem("scattered1")]
        xsc_ready = sem("xsc_ready")
        count_made = sem("count_made")
        table_ready = sem("table_ready")
        zeroed = sem("zeroed")
        spare_zeroed = sem("spare_zeroed")
        slot_in = [sem("slot_in0"), sem("slot_in1")]
        slot_out = [sem("slot_out0"), sem("slot_out1")]
        gathered = [sem(f"gathered{j}") for j in range(TB)]
        v_final = sem("v_final")
        edif_ready = sem("edif_ready")
        out_ready = sem("out_ready")
        stored = sem("stored")
        passed = {nc.scalar: sem("passed_act"), nc.vector: sem("passed_dve"), nc.gpsimd: sem("passed_pool")}

        PAIRS = N // 2

        def alone(engine):
            engine.sem_inc(passed[engine], 1)

        block = ctx.enter_context(nc.Block())

        def gu(e, k, c):
            if isinstance(e, int):
                a = (e * H + k) * F2 + c * F
                return wgu[:, a:a + F]
            return wgu[:, ds(e * (H * F2) + (k * F2 + c * F), F)]

        @block.sync
        def _(sp):
            def small(dst, src):
                sp.dma_start(dst, src).then_inc(small_in, 16)

            small(wx, x_proj_w[0:R, :])
            for i in range(PARTS):
                small(wbc[i * BC:(i + 1) * BC, :], x_proj_w[R:R + BC, :])
            small(dtw, dt_w.rearrange("(h p) r -> p h r", p=P))
            small(alog[:], a_log.rearrange("(h p) n -> p h n", p=P))
            with nc.allow_non_contiguous_dma(reason="two columns of 128 scalars"):
                small(dsk[:], d_skip.rearrange("(h p) -> p h", p=P))
                small(dtb[:], dt_b.rearrange("(h p) -> p h", p=P))
            small(gw[:], gate_w.rearrange("(k p) e -> p k e", p=P))
            sp.dma_start(xs, x_view[:, 0:TB, :]).then_inc(x_in, 16)
            with sp.Fori(1, NB) as b:
                sp.wait_ge(x_turned, b)
                sp.dma_start(xs, x_view[:, ds(b * TB, TB), :]).then_inc(x_in, 16)
            gu_view = wgu[:].rearrange("p (e k f) -> p e k f", e=E + 1, k=H)
            sp.dma_start(gu_view[:, E], ws_gu.rearrange("(k p) f -> p k f", p=P)).then_inc(shared_in, 16)
            sp.dma_start(wds[:].rearrange("p (k d) -> p k d", k=KF),
                         ws_dn.rearrange("(k p) d -> p k d", p=P)).then_inc(shared_in, 16)
            for e in range(E):
                sp.dma_start(gu_view[:, e], w_gu[e].rearrange("(k p) f -> p k f", p=P)).then_inc(gu_in, 16)
            sp.wait_ge(consts, 1)
            for i in range(SPARE):
                sp.dma_start(slots[E * REGION + i * P:E * REGION + (i + 1) * P, :],
                             zeros[:]).then_inc(spare_zeroed, 16)
            sp.wait_ge(x1_ready, NT)
            sp.wait_ge(y_added, NB * N)
            dn_view = wdn.rearrange("p (e k d) -> p e k d", e=E, k=KF)
            for e in range(E):
                sp.dma_start(dn_view[:, e], w_dn[e].rearrange("(k p) d -> p k d", p=P)).then_inc(dn_in, 16)
            sp.wait_ge(table_ready, 1)
            for e in range(E):
                n = sp.value_load(cnti[0:1, e:e + 1], min_val=0, max_val=NT * P)
                sp.dma_start(slots[ds(n + e * REGION, P), :], zeros[:]).then_inc(zeroed, 16)
            sp.wait_ge(zeroed, 16 * E)
            sp.wait_ge(spare_zeroed, 16 * SPARE)
            for s in range(2):
                sp.wait_ge(scattered[s], 16 * TOP * (NT // 2))

            def page(j):
                return sp.value_load(tab_r[0:1, ds(j, 1)], min_val=0, max_val=ROWS - P)

            def load(j, s):
                sp.dma_start(x1s[:, s, :], slots[ds(page(j), P), :]).then_inc(slot_in[s], 16)

            def store(j, s):
                sp.dma_start(slots_y[ds(j * P, P), :] if not isinstance(j, int) else slots_y[j * P:(j + 1) * P, :],
                             yo[:, s, :]).then_inc(slot_out[s], 16)

            load(0, 0)
            load(1, 1)
            sp.wait_ge(X_turned, NT + 1)
            load(2, 0)
            sp.wait_ge(X_turned, NT + 2)
            load(3, 1)
            sp.wait_ge(O_read, NT + 1)
            store(0, 0)
            with sp.Fori(1, RT // 2 - 1) as i:
                for s in range(2):
                    sp.wait_ge(O_read, i * 2 + (NT + s))
                    store(i * 2 + (s - 1), 1 - s)
                    sp.wait_ge(X_turned, i * 2 + (NT + 1 + s))
                    load(i * 2 + (2 + s), s)
            for j in range(RT - 3, RT):
                sp.wait_ge(O_read, NT + 1 + j)
                store(j, j % 2)

        @block.gpsimd
        def _(pool):
            step = Chain(pool, pool_steps)
            nc.gpsimd.memset(zeros[:], 0.0).then_inc(consts, 1)
            step.link(nc.gpsimd.memset(ident[:], 0.0))
            step.link(nc.gpsimd.affine_select(out=ident[:], in_=ident[:], compare_op=ALU.not_equal, fill=1.0,
                                              base=0, pattern=[[-1, P]], channel_multiplier=1))
            step.link(nc.gpsimd.memset(ones[:], 1.0))
            step.link(nc.gpsimd.affine_select(out=tri[:], in_=ones[:], compare_op=ALU.is_gt, fill=0.0,
                                              base=0, pattern=[[1, P]], channel_multiplier=-1))
            step.link(nc.gpsimd.memset(sel[:], 0.0))
            for i in range(PARTS):
                step.link(nc.gpsimd.affine_select(out=sel[:], in_=sel[:], compare_op=ALU.not_equal, fill=1.0,
                                                  base=-i * BC, pattern=[[-1, BC], [0, P]],
                                                  channel_multiplier=1))
            step.link(nc.gpsimd.iota(iota8[:], pattern=[[1, E]], base=0, channel_multiplier=0,
                                     allow_small_or_imprecise_dtypes=True))
            step.link(nc.gpsimd.iota(base8[:], pattern=[[REGION, E]], base=0, channel_multiplier=0,
                                     allow_small_or_imprecise_dtypes=True))
            step.link(nc.gpsimd.iota(jrow[:], pattern=[[1, RT]], base=0, channel_multiplier=0,
                                     allow_small_or_imprecise_dtypes=True))
            step.link(nc.gpsimd.iota(jbase[:], pattern=[[P, RT]], base=0, channel_multiplier=0,
                                     allow_small_or_imprecise_dtypes=True))
            step.link(nc.gpsimd.memset(cum[:], 0.0))
            nc.gpsimd.memset(onerow[:], 1.0).then_inc(consts, 1)

            def scatter(t, s, i):
                if not isinstance(i, int):
                    pool.wait_ge(scattered[s], i * (16 * TOP))
                nc.gpsimd.tensor_copy(xsc[:, s, :], x1[:, ds(t, 1), :].rearrange("p o d -> p (o d)")
                                      ).then_inc(xsc_ready, 1)
                pool.wait_ge(xsc_ready, t + 1)
                pool.wait_ge(idx_ready, t + 1)
                alone(pool)
                for k in range(TOP):
                    pool.indirect_dma_start(
                        out=slots[:, :], out_offset=bass.IndirectOffsetOnAxis(ap=idx_now[:, s, k:k + 1], axis=0),
                        in_=xsc[:, s, :], in_offset=None).then_inc(scattered[s], 16)

            pool.wait_ge(x1_ready, NT)
            pool.wait_ge(y_added, NB * N)
            scatter(0, 0, 0)
            scatter(1, 1, 0)
            with pool.Fori(1, NT // 2) as i:
                scatter(i * 2, 0, i)
                scatter(i * 2 + 1, 1, i)
            pool.wait_ge(idx_ready, NT + 1)
            pool.wait_ge(slot_out[0], 16 * (RT // 2))
            pool.wait_ge(slot_out[1], 16 * (RT // 2))
            for t in range(NT):
                j = t % TB
                if t >= TB:
                    pool.wait_ge(v_final, t - TB + 1)
                for k in range(TOP):
                    pool.indirect_dma_start(
                        out=gat[:, j, k, :], out_offset=None, in_=slots_y[:, :],
                        in_offset=bass.IndirectOffsetOnAxis(ap=idx_all[:, t * TOP + k:t * TOP + k + 1], axis=0),
                    ).then_inc(gathered[j], 16)

        @block.tensor
        def _(pe):
            pe.wait_ge(small_in, 16 * 9)
            pe.wait_ge(consts, 2)
            for k in range(H):
                nc.tensor.transpose(bank[0][:, k * P:(k + 1) * P], wx[:, k * P:(k + 1) * P], ident[:])
                nc.tensor.transpose(bank[0][:, (2 + k) * P:(3 + k) * P], dtw[:, k, :], ident[:])
                last = nc.tensor.transpose(bank[1][:, k * P:k * P + PARTS * BC], wbc[:, k * P:(k + 1) * P],
                                           ident[0:PARTS * BC, 0:PARTS * BC])
            last.then_inc(wT_made, 1)
            pe.wait_ge(wT_ready, 2)

            def prepare(b, first):
                pe.wait_ge(x_in, b * 16 + 16)
                if not first:
                    pe.wait_ge(dr_made, b)
                for h in range(H):
                    for j in range(TB):
                        last = nc.tensor.transpose(bank[h][:, j * P:(j + 1) * P],
                                                   xs[:, j, h * P:(h + 1) * P], ident[:])
                last.then_inc(x_turned, 1)
                pe.wait_ge(xT_act, b + 1)
                pe.wait_ge(xT_dve, b + 1)
                if not first:
                    pe.wait_ge(dr_kept, b)
                for k in range(H):
                    last = nc.tensor.matmul(bank[2][:], wT[:, k * P:(k + 1) * P], xT[:, k, ds(b * L, L)],
                                            start=k == 0, stop=k == H - 1)
                last.then_inc(dr_made, 1)
                if not first:
                    pe.wait_ge(bc_read, b)
                for k in range(H):
                    last = nc.tensor.matmul(bank[3][0:PARTS * BC, :], wbcT[:, k, :], xT[:, k, ds(b * L, L)],
                                            start=k == 0, stop=k == H - 1)
                last.then_inc(bc_made, 1)
                pe.wait_ge(dr_kept, b + 1)
                if not first:
                    pe.wait_ge(prep_done, b)
                for h in range(H):
                    last = nc.tensor.matmul(bank[4 + h][:], wT[:, (2 + h) * P:(3 + h) * P], drT,
                                            start=True, stop=True)
                last.then_inc(z_made, 1)

            prepare(0, True)
            with pe.Fori(1, NB) as b:
                prepare(b, False)
            pe.wait_ge(prep_done, NB)

            def spread(b, n, g, first):
                s = first[1]
                if not first[0]:
                    pe.wait_ge(dBu_ready, g - 1)
                nc.tensor.matmul(psB[s][:], sel[:, n, :], stack[:, ds(b * L, L)],
                                 start=True, stop=True).then_inc(B_ready, 1)
                if not first[0]:
                    pe.wait_ge(hC_ready, g - 1)
                nc.tensor.matmul(psC[s][:], sel[:, N + n if isinstance(n, int) else n + N, :],
                                 stack[:, ds(b * L, L)], start=True, stop=True).then_inc(C_ready, 1)

            def add_y(g, s, start=False, stop=False):
                pe.wait_ge(hC_ready, g + 1)
                for h in range(H):
                    last = nc.tensor.matmul(psY[h][:], ident[:], hC[:, s, h, :], start=start, stop=stop)
                last.then_inc(y_added, 1)

            def scan_batch(b, g0, first):
                spread(b, 0, g0, (first, 0))
                spread(b, 1, g0 + 1, (first, 1))
                spread(b, 2, g0 + 2, (False, 0))
                if not first:
                    pe.wait_ge(v_ready, b)
                add_y(g0, 0, start=True)
                spread(b, 3, g0 + 3, (False, 1))
                add_y(g0 + 1, 1)
                for i in range(2, PAIRS):
                    for s in range(2):
                        spread(b, 2 * i + s, g0 + (2 * i + s), (False, s))
                        add_y(g0 + (2 * i + s - 2), s)
                add_y(g0 + (N - 2), 0)
                add_y(g0 + (N - 1), 1, stop=True)
                pe.wait_ge(v_ready, b + 1)
                if not first:
                    pe.wait_ge(x1_ready, b * TB)
                for j in range(TB):
                    for h in range(H):
                        last = nc.tensor.transpose(psV[j // 2][:, (j % 2) * D + h * P:(j % 2) * D + (h + 1) * P],
                                                   vb[:, h, j * P:(j + 1) * P], ident[:])
                last.then_inc(v_turned, 1)

            scan_batch(0, 0, True)
            with pe.Fori(1, NB) as b:
                scan_batch(b, b * N, False)

            def turn_x(u, s):
                for k in range(H):
                    last = nc.tensor.transpose(psX[:, k * P:(k + 1) * P], x1s[:, s, k * P:(k + 1) * P], ident[:])
                last.then_inc(X_turned, 1)

            def gate_or_up(e, c, s, done):
                bank_of = (psG, psU)[c]
                for k in range(H):
                    last = nc.tensor.matmul(bank_of[:], xTs[:, s, k, :], gu(e, k, c), start=k == 0, stop=k == H - 1)
                last.then_inc(done, 1)

            def turn_h(u):
                pe.wait_ge(hp_ready, u + 1)
                for k in range(KF):
                    last = nc.tensor.transpose(psH[:, k * P:(k + 1) * P], hp[:, k * P:(k + 1) * P], ident[:])
                last.then_inc(H_turned, 1)

            def down(u, w):
                pe.wait_ge(hT_ready, u + 1)
                pe.wait_ge(O_read, u)
                for k in range(KF):
                    last = nc.tensor.matmul(psO[:, 0:D], hT[:, k, :], w(k), start=k == 0, stop=k == KF - 1)
                last.then_inc(O_made, 1)

            def logits(t, s):
                pe.wait_ge(XT_ready, t + 1)
                pe.wait_ge(L_read, t)
                for k in range(H):
                    last = nc.tensor.matmul(psL[:, 0:E], xTs[:, s, k, :], gw[:, k, :], start=k == 0, stop=k == H - 1)
                last.then_inc(L_made, 1)

            def ranks(t, s):
                pe.wait_ge(mask_ready, t + 1)
                pe.wait_ge(idx_ready, t)
                nc.tensor.matmul(psR[:, 0:E], tri[:], mask[:, s, :], start=True, stop=False)
                nc.tensor.matmul(psR[:, 0:E], ones[:], cum[:, s, :], start=False, stop=True).then_inc(rank_made, 1)

            def w_shared(k):
                return wds[:, k * D:(k + 1) * D]

            def shared_tile(t, s, first, last):
                pe.wait_ge(XT_ready, t + 1)
                if not first:
                    pe.wait_ge(silu_done, t)
                gate_or_up(E, 0, s, G_made)
                if not first:
                    turn_h(t - 1)
                if not last:
                    pe.wait_ge(x1_copied, t + 2)
                    turn_x(t + 1, 1 - s)
                gate_or_up(E, 1, s, U_made)
                if not first:
                    down(t - 1, w_shared)
                if not last:
                    logits(t + 1, 1 - s)
                ranks(t, s)

            pe.wait_ge(shared_in, 32)
            pe.wait_ge(x1_ready, NT)
            pe.wait_ge(x1_copied, 1)
            turn_x(0, 0)
            logits(0, 0)
            shared_tile(0, 0, True, False)
            shared_tile(1, 1, False, False)
            with pe.Fori(1, NT // 2 - 1) as i:
                shared_tile(i * 2, 0, False, False)
                shared_tile(i * 2 + 1, 1, False, False)
            shared_tile(NT - 2, 0, False, False)
            shared_tile(NT - 1, 1, False, True)
            pe.wait_ge(idx_ready, NT)
            nc.tensor.matmul(psR[:, 0:E], ones[:], cum[:, NT % 2, :], start=True, stop=True).then_inc(count_made, 1)
            turn_h(NT - 1)
            down(NT - 1, w_shared)

            def expert_of(j):
                return pe.value_load(tab_e[0:1, ds(j, 1)], min_val=0, max_val=E - 1)

            def w_of(e):
                return lambda k: wdn[:, ds(e * (KF * D) + k * D, D)]

            def routed_tile(j, s, before, loads, first=False, last=False):
                e = expert_of(j)
                pe.wait_ge(XT_ready, j + (NT + 1))
                gate_or_up(e, 0, s, G_made)
                if not first:
                    turn_h(j + (NT - 1))
                if not last:
                    pe.wait_ge(slot_in[1 - s], loads * 16)
                    turn_x(None, 1 - s)
                gate_or_up(e, 1, s, U_made)
                if not first:
                    down(j + (NT - 1), w_of(before))
                return e

            pe.wait_ge(table_ready, 1)
            pe.wait_ge(gu_in, 16 * E)
            pe.wait_ge(dn_in, 16 * E)
            pe.wait_ge(slot_in[0], 16)
            turn_x(None, 0)
            e = routed_tile(0, 0, None, 1, first=True)
            e = routed_tile(1, 1, e, 2)
            with pe.Fori(1, RT // 2 - 1) as i:
                e = routed_tile(i * 2, 0, expert_of(i * 2 - 1), i + 1)
                e = routed_tile(i * 2 + 1, 1, e, i + 2)
            e = routed_tile(RT - 2, 0, expert_of(RT - 3), RT // 2)
            e = routed_tile(RT - 1, 1, e, None, last=True)
            turn_h(NT + RT - 1)
            down(NT + RT - 1, w_of(e))

        @block.scalar
        def _(act):
            step = Chain(act, s_steps)
            act.wait_ge(small_in, 16 * 9)
            nc.scalar.activation(aexp[:], alog[:], ACT.Exp).then_inc(a_exp, 1)
            def prepare(b, first):
                step.start(b * 2)
                act.wait_ge(x_turned, b + 1)
                alone(act)
                nc.scalar.activation(xT[:, 0, ds(b * L, L)], bank[0][:], ACT.Copy).then_inc(xT_act, 1)
                act.wait_ge(dr_made, b + 1)
                if not first:
                    act.wait_ge(z_made, b)
                nc.scalar.activation(drT, bank[2][:], ACT.Copy).then_inc(dr_kept, 1)
                act.wait_ge(zb_ready, b + 1)
                if not first:
                    act.wait_ge(prep_done, b)
                step.link(nc.scalar.activation(ab, zb, ACT.Abs))
                step.link(nc.scalar.activation(ab, ab, ACT.Exp, scale=-1.0))
                nc.scalar.activation(ab, ab, ACT.Ln, bias=1.0).then_inc(ab_ready, 1)

            prepare(0, True)
            with act.Fori(1, NB) as b:
                prepare(b, False)
            act.wait_ge(a_ready, 1)
            act.wait_ge(prep_done, NB)

            def decays(b, n, g, s, first):
                if not first:
                    act.wait_ge(h_ready, g - 1)
                    alone(act)
                for h in range(H):
                    last = nc.scalar.activation(dA[:, s, h, :], delta[:, h, ds(b * L, L)], ACT.Exp,
                                                scale=aneg[:, h, n:n + 1])
                last.then_inc(dA_ready, 1)

            def inv_std(count):
                act.wait_ge(var_ready, count)
                step.link(nc.scalar.activation(lnv[:], ve[:], ACT.Ln))
                nc.scalar.activation(r0[:], lnv[:], ACT.Exp, scale=-0.5).then_inc(rstd_ready, 1)

            def scan_batch(b, g0, first):
                for n in range(N):
                    decays(b, n, g0 + n, n % 2, first and n < 2)
                inv_std(b + 1)

            step.start(NB * 2)
            scan_batch(0, 0, True)
            with act.Fori(1, NB) as b:
                step.start(b + NB * 2)
                scan_batch(b, b * N, False)
            step.start(NB * 3)

            def copy_x1(t, s):
                nc.scalar.activation(x1s[:, s, :], x1[:, ds(t, 1), :].rearrange("p o d -> p (o d)"),
                                     ACT.Copy).then_inc(x1_copied, 1)

            def keep_xT(u, s):
                act.wait_ge(X_turned, u + 1)
                nc.scalar.activation(xTs[:, s, :, :].rearrange("p k m -> p (k m)"), psX[:, 0:D],
                                     ACT.Copy).then_inc(XT_ready, 1)

            def silu(u):
                act.wait_ge(G_made, u + 1)
                nc.scalar.activation(gs, psG[:], ACT.Silu).then_inc(silu_done, 1)

            def keep_hT(u):
                act.wait_ge(H_turned, u + 1)
                nc.scalar.activation(hT.rearrange("p k m -> p (k m)"), psH[:], ACT.Copy).then_inc(hT_ready, 1)

            def shared_tile(t, s, first, last):
                if not last:
                    if not first:
                        act.wait_ge(X_turned, t)
                        alone(act)
                    copy_x1(t + 1, 1 - s)
                if not first:
                    act.wait_ge(hp_ready, t)
                silu(t)
                if not first:
                    act.wait_ge(O_made, t - 1)
                    keep_hT(t - 1)
                if not last:
                    if not first:
                        act.wait_ge(U_made, t)
                        act.wait_ge(L_made, t)
                    keep_xT(t + 1, 1 - s)

            act.wait_ge(x1_ready, NT)
            act.wait_ge(y_added, NB * N)
            copy_x1(0, 0)
            keep_xT(0, 0)
            shared_tile(0, 0, True, False)
            shared_tile(1, 1, False, False)
            with act.Fori(1, NT // 2 - 1) as i:
                shared_tile(i * 2, 0, False, False)
                shared_tile(i * 2 + 1, 1, False, False)
            shared_tile(NT - 2, 0, False, False)
            shared_tile(NT - 1, 1, False, True)
            act.wait_ge(O_made, NT - 1)
            keep_hT(NT - 1)

            def routed_tile(u, s, first=False, last=False):
                act.wait_ge(hp_ready, u)
                silu(u)
                if not first:
                    act.wait_ge(O_made, u - 1)
                    keep_hT(u - 1)
                if not last:
                    act.wait_ge(U_made, u)
                    keep_xT(u + 1, 1 - s)

            act.wait_ge(U_made, NT)
            keep_xT(NT, 0)
            routed_tile(NT, 0, first=True)
            routed_tile(NT + 1, 1)
            with act.Fori(1, RT // 2 - 1) as i:
                routed_tile(i * 2 + NT, 0)
                routed_tile(i * 2 + (NT + 1), 1)
            routed_tile(NT + RT - 2, 0)
            routed_tile(NT + RT - 1, 1, last=True)
            act.wait_ge(O_made, NT + RT - 1)
            keep_hT(NT + RT - 1)
            act.wait_ge(idx_ready, NT)
            nc.scalar.activation(edif[:], dif[:], ACT.Exp).then_inc(edif_ready, 1)
            with act.Fori(0, NB) as b:
                step.start(b + NB * 3)
                inv_std(b + (NB + 1))
                act.wait_ge(out_ready, b + 1)
                act.dma_start(out_view[:, ds(b * TB, TB), :], ofin).then_inc(stored, 16)
            act.wait_ge(stored, 16 * NB)

        @block.vector
        def _(dve):
            step = Chain(dve, v_steps)
            V = nc.vector
            dve.wait_ge(small_in, 16 * 9)
            V.tensor_scalar(dsk1[:], dsk[:], 1.0, None, ALU.add)
            dve.wait_ge(a_exp, 1)
            V.tensor_scalar(aneg[:], aexp[:], -1.0, None, ALU.mult).then_inc(a_ready, 1)
            dve.wait_ge(wT_made, 1)
            V.tensor_copy(wT[:], bank[0][:]).then_inc(wT_ready, 1)
            V.tensor_copy(wbcT[:], bank[1][:, 0:H * P].rearrange("p (k m) -> p k m", k=H)[:, :, 0:PARTS * BC]
                          ).then_inc(wT_ready, 1)

            PREP = 5
            rest = vb[0:PARTS * BC, 0, :]
            with dve.Fori(0, NB) as b:
                step.start(b * PREP)
                dve.wait_ge(x_turned, b + 1)
                alone(dve)
                V.tensor_copy(xT[:, 1, ds(b * L, L)], bank[1][:]).then_inc(xT_dve, 1)
                dve.wait_ge(bc_made, b + 1)
                step.link(V.tensor_copy(stack[:, ds(b * L, L)], bank[3][0:PARTS * BC, :]))
                step.link(V.tensor_tensor(rest, bank[3][0:PARTS * BC, :], stack[:, ds(b * L, L)], ALU.subtract), alone)
                for i in range(1, PARTS):
                    last = V.tensor_copy(stack[i * BC:(i + 1) * BC, ds(b * L, L)], vb[i * BC:(i + 1) * BC, 0, :])
                step.link(last)
                step.link(V.tensor_tensor(vb[2 * BC:3 * BC, 1, :], vb[2 * BC:3 * BC, 0, :],
                                          stack[2 * BC:3 * BC, ds(b * L, L)], ALU.subtract), alone)
                V.tensor_copy(stack[2 * BC:3 * BC, ds(b * L, L)], vb[2 * BC:3 * BC, 1, :]).then_inc(bc_read, 1)
                dve.wait_ge(z_made, b + 1)
                for h in range(H):
                    last = V.tensor_scalar(zb[:, h, :], bank[4 + h][:], dtb[:, h:h + 1], None, ALU.add)
                last.then_inc(zb_ready, 1)
                dve.wait_ge(zb_ready, b + 1)
                dve.wait_ge(ab_ready, b + 1)
                step.link(V.scalar_tensor_tensor(delta[:, :, ds(b * L, L)], zb, 0.0, ab, ALU.max, ALU.add))
                dve.wait_ge(xT_act, b + 1)
                V.tensor_tensor(du[:, :, ds(b * L, L)], delta[:, :, ds(b * L, L)], xT[:, :, ds(b * L, L)],
                                ALU.mult).then_inc(prep_done, 1)

            def inject(b, g, n, first):
                s = n % 2
                dve.wait_ge(B_ready, g + 1)
                if not (first and n < RING):
                    dve.wait_ge(h_ready, g - (RING - 1))
                V.tensor_tensor(dBu[:, n % RING], du[:, :, ds(b * L, L)],
                                psB[s][:].unsqueeze(1).to_broadcast([P, H, L]), ALU.mult).then_inc(dBu_ready, 1)

            def scan(g, n, first):
                dve.wait_ge(dBu_ready, g + 1)
                dve.wait_ge(dA_ready, g + 1)
                if not (first and n < 2):
                    dve.wait_ge(hC_ready, g - 1)
                for h in range(H):
                    last = V.tensor_tensor_scan(hs[:, n % 2, h, :], dA[:, n % 2, h, :], dBu[:, n % RING, h, :], 0.0,
                                                ALU.mult, ALU.add)
                last.then_inc(h_ready, 1)

            def project(g, s, first):
                dve.wait_ge(h_ready, g + 1)
                dve.wait_ge(C_ready, g + 1)
                if not first:
                    dve.wait_ge(y_added, g - 1)
                V.tensor_tensor(hC[:, s], hs[:, s], psC[s][:].unsqueeze(1).to_broadcast([P, H, L]),
                                ALU.mult).then_inc(hC_ready, 1)

            def inv_std(count):
                dve.wait_ge(rstd_ready, count)
                step.link(V.tensor_tensor(r1[:], r0[:], r0[:], ALU.mult))
                step.link(V.tensor_tensor(r2[:], r1[:], ve[:], ALU.mult))
                step.link(V.tensor_scalar(r3[:], r2[:], -0.5, 1.5, ALU.mult, ALU.add))
                step.link(V.tensor_tensor(rstd[:], r0[:], r3[:], ALU.mult))

            def stats(tiles):
                for j, tile in enumerate(tiles):
                    last = V.bn_stats(st6[:, j, :], tile)
                step.link(last, alone)
                for j in range(TB):
                    last = V.bn_aggr(mv[:, j, :], st6[:, j, :])
                step.link(last)
                V.tensor_scalar(ve[:], mv[:, :, 1], EPS, None, ALU.add).then_inc(var_ready, 1)

            SCAN = 6

            def scan_batch(b, g0, first):
                inject(b, g0, 0, first)
                for n in range(N):
                    if n < N - 1:
                        inject(b, g0 + (n + 1), n + 1, first)
                    if n >= 1:
                        project(g0 + (n - 1), (n - 1) % 2, first and n < 3)
                    scan(g0 + n, n, first)
                project(g0 + (N - 1), 1, False)
                dve.wait_ge(y_added, g0 + N)
                if not first:
                    dve.wait_ge(v_turned, b)
                for h in range(H):
                    last = V.scalar_tensor_tensor(vb[:, h, :], xT[:, h, ds(b * L, L)], dsk1[:, h:h + 1],
                                                  psY[h][:], ALU.mult, ALU.add)
                last.then_inc(v_ready, 1)
                dve.wait_ge(v_turned, b + 1)
                alone(dve)
                tiles = [psV[j // 2][:, (j % 2) * D:(j % 2 + 1) * D] for j in range(TB)]
                stats(tiles)
                inv_std(b + 1)
                for j in range(TB):
                    V.tensor_scalar(x1[:, ds(b * TB + j, 1), :].rearrange("p o d -> p (o d)"), tiles[j],
                                    mv[:, j, 0:1], rstd[:, j:j + 1], ALU.subtract, ALU.mult).then_inc(x1_ready, 1)

            step.start(NB * PREP)
            scan_batch(0, 0, True)
            with dve.Fori(1, NB) as b:
                step.start(b * SCAN + NB * PREP)
                scan_batch(b, b * N, False)
            scanned = NB * (PREP + SCAN)

            def choose(t, s):
                dve.wait_ge(L_made, t + 1)
                V.tensor_copy(lg[:], psL[:, 0:E]).then_inc(L_read, 1)
                dve.wait_ge(L_read, t + 1)
                alone(dve)
                step.link(V.max(mx8[:], lg[:]), alone)
                step.link(V.max_index(ix8[:], mx8[:], lg[:]))
                V.tensor_tensor(dif[:, ds(t, 1)], mx8[:, 1:2], mx8[:, 0:1], ALU.subtract)
                step.link(V.tensor_copy(ixf[:], ix8[:, 0:TOP]))
                for k in range(TOP):
                    last = V.tensor_scalar(oh[:, s, k, :], iota8[:], ixf[:, k:k + 1], None, ALU.is_equal)
                step.link(last)
                V.tensor_tensor(mask[:, s, :], oh[:, s, 0, :], oh[:, s, 1, :], ALU.add).then_inc(mask_ready, 1)

            def place(t, s):
                dve.wait_ge(rank_made, t + 1)
                step.link(V.tensor_tensor(cum[:, 1 - s, :], cum[:, s, :], mask[:, s, :], ALU.add))
                step.link(V.tensor_tensor(rank8[:], psR[:, 0:E], base8[:], ALU.add))
                for k in range(TOP):
                    last = V.tensor_tensor(pick[:, k, :], oh[:, s, k, :], rank8[:], ALU.mult)
                step.link(last)
                step.link(V.tensor_reduce(slotf[:], pick[:], AX.X, ALU.add), alone)
                V.tensor_copy(slot_all[:, ds(t * TOP, TOP)], slotf[:])
                V.tensor_copy(ex_all[:, ds(t * TOP, TOP)], ixf[:])
                V.tensor_copy(idx_now[:, s, :], slotf[:]).then_inc(idx_ready, 1)

            def product(u):
                dve.wait_ge(silu_done, u + 1)
                dve.wait_ge(U_made, u + 1)
                V.tensor_tensor(hp, gs, psU[:], ALU.mult).then_inc(hp_ready, 1)

            def add_shared(t):
                dve.wait_ge(O_made, t + 1)
                dve.wait_ge(xsc_ready, t + 1)
                row = x1[:, ds(t, 1), :].rearrange("p o d -> p (o d)")
                V.tensor_tensor(row, row, psO[:, 0:D], ALU.add).then_inc(O_read, 1)

            TILE = 8

            def shared_tile(t, s, i, first=False):
                choose(t, s)
                if not first:
                    dve.wait_ge(H_turned, t)
                product(t)
                if not first:
                    add_shared(t - 1)
                if not isinstance(i, int):
                    dve.wait_ge(scattered[s], i * (16 * TOP))
                place(t, s)

            step.start(scanned)
            shared_tile(0, 0, 0, first=True)
            shared_tile(1, 1, 0)
            with dve.Fori(1, NT // 2) as i:
                step.start(i * (2 * TILE) + scanned)
                shared_tile(i * 2, 0, i)
                shared_tile(i * 2 + 1, 1, i)
            step.start(scanned + NT * TILE)
            dve.wait_ge(count_made, 1)
            step.link(V.tensor_copy(cnt[:], psR[:, 0:E]))
            step.link(V.tensor_copy(cnti[:], cnt[:]))
            step.link(V.tensor_scalar(pgi[:], cnt[:], float(P - 1), None, ALU.add))
            step.link(V.tensor_single_scalar(pgs[:], pgi[:], P.bit_length() - 1, ALU.arith_shift_right))
            step.link(V.tensor_copy(pages[:], pgs[:]))
            step.link(V.tensor_tensor_scan(ends[:], onerow[:], pages[:], 0.0, ALU.mult, ALU.add))
            step.link(V.tensor_scalar(skip[:], pages[:], -float(P), float(REGION), ALU.mult, ALU.add))
            step.link(V.tensor_tensor(past, jrow[:].unsqueeze(2).to_broadcast([1, RT, E]),
                                      ends[0:1, :].unsqueeze(1).to_broadcast([1, RT, E]), ALU.is_ge))
            step.link(V.tensor_tensor(jump, past, skip[0:1, :].unsqueeze(1).to_broadcast([1, RT, E]), ALU.mult))
            step.link(V.tensor_reduce(esum[:], past, AX.X, ALU.add))
            step.link(V.tensor_reduce(rsum[:], jump, AX.X, ALU.add))
            step.link(V.tensor_tensor(rowf[:], rsum[:], jbase[:], ALU.add))
            step.link(V.tensor_copy(tab_r[:], rowf[:]))
            V.tensor_scalar(tab_e[:], esum[:], float(E - 1), None, ALU.min).then_inc(table_ready, 1)
            step.link(V.tensor_tensor(starts[:], ends[:], pages[:], ALU.subtract))
            step.link(V.scalar_tensor_tensor(shift[:], starts[:], -float(P), base8[:], ALU.mult, ALU.add))
            step.link(V.tensor_tensor(is_ex, ex_all[:].unsqueeze(2).to_broadcast([P, NT * TOP, E]),
                                      iota8[:].unsqueeze(1).to_broadcast([P, NT * TOP, E]), ALU.is_equal))
            step.link(V.tensor_tensor(moved, is_ex, shift[:].unsqueeze(1).to_broadcast([P, NT * TOP, E]),
                                      ALU.mult))
            step.link(V.tensor_reduce(back[:], moved, AX.X, ALU.add))
            step.link(V.tensor_tensor(row_y[:], slot_all[:], back[:], ALU.subtract))
            V.tensor_copy(idx_all[:], row_y[:]).then_inc(idx_ready, 1)
            add_shared(NT - 1)

            def keep_y(u, s, stores):
                dve.wait_ge(O_made, u + 1)
                if stores is not None:
                    dve.wait_ge(slot_out[s], stores * 16)
                V.tensor_copy(yo[:, s, :], psO[:, 0:D]).then_inc(O_read, 1)

            def routed_tile(u, s, stores, first=False):
                dve.wait_ge(H_turned, u)
                product(u)
                if not first:
                    keep_y(u - 1, 1 - s, stores)

            routed_tile(NT, 0, None, first=True)
            routed_tile(NT + 1, 1, None)
            routed_tile(NT + 2, 0, None)
            routed_tile(NT + 3, 1, 1)
            with dve.Fori(2, RT // 2) as i:
                routed_tile(i * 2 + NT, 0, i - 1)
                routed_tile(i * 2 + (NT + 1), 1, i)
            keep_y(NT + RT - 1, 1, RT // 2 - 1)
            dve.wait_ge(edif_ready, 1)
            step.link(V.tensor_scalar(eden[:], edif[:], 1.0, None, ALU.add))
            step.link(V.reciprocal(wt0[:], eden[:]))
            step.link(V.tensor_tensor(wt1[:], wt0[:], edif[:], ALU.mult))
            head = scanned + NT * TILE + step.n

            FIN = 1 + SCAN

            def finish(b, first):
                step.start(b * FIN + head)
                for j in range(TB):
                    dve.wait_ge(gathered[j], b * (16 * TOP) + 16 * TOP)
                    row = x1[:, ds(b * TB + j, 1), :].rearrange("p o d -> p (o d)")
                    last = V.scalar_tensor_tensor(row, gat[:, j, 0, :], wt0[:, ds(b * TB + j, 1)], row,
                                                  ALU.mult, ALU.add)
                step.link(last)
                for j in range(TB):
                    row = x1[:, ds(b * TB + j, 1), :].rearrange("p o d -> p (o d)")
                    V.scalar_tensor_tensor(vfin[:, j, :], gat[:, j, 1, :], wt1[:, ds(b * TB + j, 1)], row,
                                           ALU.mult, ALU.add).then_inc(v_final, 1)
                dve.wait_ge(v_final, b * TB + TB)
                alone(dve)
                stats([vfin[:, j, :] for j in range(TB)])
                inv_std(b + (NB + 1))
                if not first:
                    dve.wait_ge(stored, b * 16)
                for j in range(TB):
                    last = V.tensor_scalar(ofin[:, j, :], vfin[:, j, :], mv[:, j, 0:1], rstd[:, j:j + 1],
                                           ALU.subtract, ALU.mult)
                last.then_inc(out_ready, 1)

            finish(0, True)
            with dve.Fori(1, NB) as b:
                finish(b, False)


_INS = ["L0_attn_x", "L0_attn_A_log", "L0_attn_D", "L0_attn_x_proj_w", "L0_attn_dt_proj_w", "L0_attn_dt_proj_b",
        "L0_ffn_gate_w", "L0_ffn_w_gate_up", "L0_ffn_w_down", "L0_ffn_shared_gate_up", "L0_ffn_shared_down"]


def kernel(**inputs):
    import numpy as _np
    import concourse.bacc as _bacc
    from concourse import mybir as _mybir
    from concourse.bass_utils import run_bass_kernel_spmd as _run

    nc = _bacc.Bacc("TRN2", target_bir_lowering=False, num_devices=1)
    arrays, args = {}, []
    for name in _INS:
        a = _np.ascontiguousarray(inputs[name])
        arrays[f"in_{name}"] = a
        args.append(nc.dram_tensor(f"in_{name}", a.shape, _mybir.dt.from_np(a.dtype), kind="ExternalInput").ap())
    out = nc.dram_tensor("out_0", inputs["L0_attn_x"].shape, _mybir.dt.float32, kind="ExternalOutput").ap()
    mamba_moe(nc, *args, out)
    r = _run(nc, [arrays], core_ids=[0])
    return r.results[0]["out_0"]
```

```python
from contextlib import ExitStack

import concourse.bass as bass
from concourse import mybir

ALU = mybir.AluOpType
ACT = mybir.ActivationFunctionType
F32 = mybir.dt.float32
BF16 = mybir.dt.bfloat16
I32 = mybir.dt.int32
U32 = mybir.dt.uint32
AX = mybir.AxisListType
ds = bass.ds

POOL_OF = 4
P = 128
EPS = 1e-5


class Chain:

    def __init__(self, engine, sem):
        self.engine, self.sem, self.base, self.n = engine, sem, 0, 0

    def link(self, instruction, alone=None):
        self.n += 1
        instruction.then_inc(self.sem, 1)
        self.engine.wait_ge(self.sem, self.base + self.n)
        if alone:
            alone(self.engine)

    def start(self, base):
        self.base, self.n = base, 0


def mamba_moe(nc, x, a_log, d_skip, x_proj_w, dt_w, dt_b, gate_w, w_gu, w_dn, ws_gu, ws_dn, out):
    NB, L, D = x.shape
    N = a_log.shape[1]
    R = dt_w.shape[1]
    E, _, F2 = w_gu.shape
    F = F2 // 2
    H = D // P
    NT = NB * L // P
    TB = L // P
    KF = F // P
    TOP = 2
    BC = 2 * N
    PARTS = 3
    RT = (NT * P * TOP + E * (P - 1)) // P
    RT += RT % 2
    REGION = NT * P + P
    SPARE = RT - NT * TOP
    ROWS = E * REGION + SPARE * P
    assert H == 2 and R == P and L == 512 and F == 512 and E == 8 and N == 16

    slots = nc.dram_tensor("slots_x", (ROWS, D), F32, kind="Internal").ap()
    slots_y = nc.dram_tensor("slots_y", (RT * P, D), F32, kind="Internal").ap()
    x_view = x.rearrange("b (j p) d -> p (b j) d", p=P)
    out_view = out.rearrange("b (j p) d -> p (b j) d", p=P)

    with ExitStack() as ctx:
        def sb(name, shape, dt=F32):
            return ctx.enter_context(nc.sbuf_tensor(name, shape, dt))

        def sem(name):
            return ctx.enter_context(nc.semaphore(name))

        wgu = sb("wgu", [P, (E + 1) * H * F2])
        wds = sb("wds", [P, KF * D])
        both = sb("both", [P, NB * H * L])
        xT = both[:].rearrange("p (b h l) -> p b h l", b=NB, h=H)
        total = both[:].rearrange("p (t d) -> p t d", d=D)
        stack = sb("stack", [PARTS * BC, NB * L], BF16)
        sel = sb("sel", [PARTS * BC, BC, P], BF16)
        vx = sb("vx", [P, H * L])
        vb = vx[:].rearrange("p (h l) -> p h l", h=H)
        x1b = vx[:].rearrange("p (j d) -> p j d", j=TB)
        xTb = sb("xTb", [P, TB, H, P])
        sg = sb("sg", [P, F])
        hp = sb("hp", [P, F])
        hT = sb("hT", [P, KF, P])
        ident = sb("ident", [P, P])
        tri = sb("tri", [P, P], BF16)
        ones = sb("ones", [P, P], BF16)
        zeros = sb("zeros", [P, D])
        wT = sb("wT", [P, 4 * P])
        wbcT = sb("wbcT", [P, H, PARTS * BC])
        alog = sb("alog", [P, H, N])
        aexp = sb("aexp", [P, H, N])
        aneg = sb("aneg", [P, H, N])
        dsk = sb("dsk", [P, H])
        dsk1 = sb("dsk1", [P, H])
        dtb = sb("dtb", [P, H])
        gw = sb("gw", [P, H, E])
        st6 = sb("st6", [P, TB, 6])
        mv = sb("mv", [P, TB, 2])
        ve = sb("ve", [P, TB])
        lnv = sb("lnv", [P, TB])
        r0 = sb("r0", [P, TB])
        r1 = sb("r1", [P, TB])
        r2 = sb("r2", [P, TB])
        r3 = sb("r3", [P, TB])
        rstd = sb("rstd", [P, TB])
        iota8 = sb("iota8", [P, E])
        base8 = sb("base8", [P, E])
        lg = sb("lg", [P, TB, E])
        mx8 = sb("mx8", [P, TB, 8])
        ix8 = sb("ix8", [P, TB, 8], U32)
        ixf = sb("ixf", [P, TB, TOP])
        oh = sb("oh", [P, TB * TOP, E])
        mask = sb("mask", [P, TB, E], BF16)
        cum = sb("cum", [P, E], BF16)
        new8 = sb("new8", [P, E])
        rank8 = sb("rank8", [P, TB, E])
        pick = sb("pick", [P, TB * TOP, E])
        slotf = sb("slotf", [P, TB * TOP])
        idx_all = sb("idx_all", [P, NT * TOP], U32)
        idx_now = sb("idx_now", [P, TB * TOP], U32)
        slot_all = sb("slot_all", [P, NT * TOP])
        ex_all = sb("ex_all", [P, NT * TOP])
        starts = sb("starts", [P, E])
        shift = sb("shift", [P, E])
        back = sb("back", [P, NT * TOP])
        row_y = sb("row_y", [P, NT * TOP])
        dif = sb("dif", [P, NT])
        edif = sb("edif", [P, NT])
        eden = sb("eden", [P, NT])
        wt0 = sb("wt0", [P, NT])
        wt1 = sb("wt1", [P, NT])
        cnt = sb("cnt", [P, E])
        cnti = sb("cnti", [P, E], I32)
        pgi = sb("pgi", [P, E], I32)
        pgs = sb("pgs", [P, E], I32)
        pages = sb("pages", [P, E])
        onerow = sb("onerow", [P, E])
        ends = sb("ends", [P, E])
        skip = sb("skip", [P, E])
        jrow = sb("jrow", [1, RT])
        jbase = sb("jbase", [1, RT])
        esum = sb("esum", [1, RT])
        rsum = sb("rsum", [1, RT])
        rowf = sb("rowf", [1, RT])
        tab_e = sb("tab_e", [1, RT], I32)
        tab_r = sb("tab_r", [1, RT], I32)

        RING = 4
        ROOM = 2 * H * L * 3 + RING * (H + 1) * L + 2 * H * NB * L
        arena = sb("arena", [P, ROOM])
        at = [0]

        def room(n):
            at[0] += n
            assert at[0] <= ROOM
            return arena[:, at[0] - n:at[0]]

        dA = room(2 * H * L).rearrange("p (s h l) -> p s h l", s=2, h=H)
        dBu = room(RING * H * L).rearrange("p (s h l) -> p s h l", s=RING, h=H)
        Bs = room(RING * L).rearrange("p (s l) -> p s l", s=RING)
        h_at = at[0]
        hs = room(2 * H * L).rearrange("p (s h l) -> p s h l", s=2, h=H)
        hC = room(2 * H * L).rearrange("p (s h l) -> p s h l", s=2, h=H)
        delta = room(NB * H * L).rearrange("p (b h l) -> p b h l", b=NB, h=H)
        du = room(NB * H * L).rearrange("p (b h l) -> p b h l", b=NB, h=H)
        at[0] = 0
        wx = room(D)
        wbc = room(D)[0:PARTS * BC, :]
        dtw = room(H * R).rearrange("p (h r) -> p h r", h=H)
        at[0] = h_at
        xs = room(TB * D).rearrange("p (j d) -> p j d", j=TB)
        drT = room(L)
        ab = room(H * L).rearrange("p (h l) -> p h l", h=H)
        zb = room(H * L).rearrange("p (h l) -> p h l", h=H)
        PAGES = 4
        at[0] = 0
        wdn = room(E * KF * D)
        page_in = room(PAGES * D).rearrange("p (s d) -> p s d", s=PAGES)
        xTs = room(2 * D).rearrange("p (s k m) -> p s k m", s=2, k=H)
        yo = room(2 * D).rearrange("p (s d) -> p s d", s=2)
        gat = room(TB * TOP * D).rearrange("p (j k d) -> p j k d", j=TB, k=TOP)
        vfin = room(TB * D).rearrange("p (j d) -> p j d", j=TB)
        ofin = room(TB * D).rearrange("p (j d) -> p j d", j=TB)
        is_ex = room(NT * TOP * E).rearrange("p (t e) -> p t e", e=E)
        moved = room(NT * TOP * E).rearrange("p (t e) -> p t e", e=E)
        past = room(RT * E)[0:1, :].rearrange("p (t e) -> p t e", e=E)
        jump = room(RT * E)[0:1, :].rearrange("p (t e) -> p t e", e=E)

        bank = [ctx.enter_context(nc.psum_tensor(f"bank{i}", [P, 512], F32)) for i in range(8)]
        psB, psC, psY, psG, psU, psM = bank[0], bank[1:3], bank[3:5], bank[5], bank[6], bank[7]
        psL = psM[:, 0:TB * E]
        psT = [(psG, psU)[j // 2][:, (j % 2) * D:(j % 2 + 1) * D] for j in range(TB)]
        psX = bank[0]
        psO = bank[1]

        small_in = sem("small_in")
        x_in = sem("x_in")
        shared_in = sem("shared_in")
        gu_in = sem("gu_in")
        dn_in = sem("dn_in")
        consts = sem("consts")
        pool_steps = sem("pool_steps")
        wT_made = sem("wT_made")
        wT_ready = sem("wT_ready")
        a_exp = sem("a_exp")
        a_ready = sem("a_ready")
        x_turned = sem("x_turned")
        xT_act = sem("xT_act")
        xT_dve = sem("xT_dve")
        dr_made = sem("dr_made")
        bc_made = sem("bc_made")
        dr_kept = sem("dr_kept")
        bc_read = sem("bc_read")
        z_made = sem("z_made")
        zb_ready = sem("zb_ready")
        ab_ready = sem("ab_ready")
        prep_done = sem("prep_done")
        v_steps = sem("v_steps")
        s_steps = sem("s_steps")
        B_ready = sem("B_ready")
        C_ready = sem("C_ready")
        dBu_ready = sem("dBu_ready")
        dA_ready = sem("dA_ready")
        h_ready = sem("h_ready")
        hC_ready = sem("hC_ready")
        y_added = sem("y_added")
        v_ready = sem("v_ready")
        v_turned = sem("v_turned")
        var_ready = sem("var_ready")
        rstd_ready = sem("rstd_ready")
        x1_ready = sem("x1_ready")
        B_kept = sem("B_kept")
        pool_dBu = sem("pool_dBu")
        X_turned = sem("X_turned")
        XT_ready = sem("XT_ready")
        L_made = sem("L_made")
        G_made = sem("G_made")
        U_made = sem("U_made")
        tanh_done = sem("tanh_done")
        silu_done = sem("silu_done")
        hp_ready = sem("hp_ready")
        H_turned = sem("H_turned")
        hT_ready = sem("hT_ready")
        O_made = sem("O_made")
        O_read = sem("O_read")
        L_read = sem("L_read")
        mask_ready = sem("mask_ready")
        rank_made = sem("rank_made")
        idx_ready = sem("idx_ready")
        scattered = sem("scattered")
        count_made = sem("count_made")
        table_ready = sem("table_ready")
        zeroed = sem("zeroed")
        spare_zeroed = sem("spare_zeroed")
        slot_in = [sem(f"slot_in{i}") for i in range(PAGES)]
        page_turned = sem("page_turned")
        page_kept = sem("page_kept")
        y_read = sem("y_read")
        add_done = sem("add_done")
        cum_ready = sem("cum_ready")
        slot_out = [sem("slot_out0"), sem("slot_out1")]
        gathered = [sem(f"gathered{j}") for j in range(TB)]
        v_final = sem("v_final")
        edif_ready = sem("edif_ready")
        out_ready = sem("out_ready")
        stored = sem("stored")
        passed = {nc.scalar: sem("passed_act"), nc.vector: sem("passed_dve"), nc.gpsimd: sem("passed_pool")}

        PAIRS = N // 2

        def alone(engine):
            engine.sem_inc(passed[engine], 1)

        block = ctx.enter_context(nc.Block())

        def gu(e, k, c):
            if isinstance(e, int):
                a = (e * H + k) * F2 + c * F
                return wgu[:, a:a + F]
            return wgu[:, ds(e * (H * F2) + (k * F2 + c * F), F)]

        BY_POOL = [n for n in range(N) if n % POOL_OF != POOL_OF - 1]
        NP, NV = len(BY_POOL), N - len(BY_POOL)

        def dBu_made(engine, b, n):
            before = sum(m in BY_POOL for m in range(n))
            if n in BY_POOL:
                engine.wait_ge(pool_dBu, b * NP + (before + 1))
            else:
                engine.wait_ge(dBu_ready, b * NV + (n - before + 1))

        def dBu_made_before(engine, b, n, back, first):
            if n >= back:
                dBu_made(engine, b, n - back)
            elif not first:
                dBu_made(engine, b - 1, n - back + N)

        def inject(engine, b, g0, n, first):
            engine.wait_ge(B_kept, g0 + (n + 1))
            if not (first and n < RING):
                engine.wait_ge(h_ready, g0 + (n - (RING - 1)))
            if n in BY_POOL:
                alone(engine)
            engine.tensor_tensor(dBu[:, n % RING], du[:, ds(b, 1)].rearrange("p o h l -> p (o h) l"),
                                 Bs[:, n % RING].unsqueeze(1).to_broadcast([P, H, L]),
                                 ALU.mult).then_inc(pool_dBu if n in BY_POOL else dBu_ready, 1)

        @block.sync
        def _(sp):
            def small(dst, src):
                sp.dma_start(dst, src).then_inc(small_in, 16)

            small(wx, x_proj_w[0:R, :])
            for i in range(PARTS):
                small(wbc[i * BC:(i + 1) * BC, :], x_proj_w[R:R + BC, :])
            small(dtw, dt_w.rearrange("(h p) r -> p h r", p=P))
            small(alog[:], a_log.rearrange("(h p) n -> p h n", p=P))
            with nc.allow_non_contiguous_dma(reason="two columns of 128 scalars"):
                small(dsk[:], d_skip.rearrange("(h p) -> p h", p=P))
                small(dtb[:], dt_b.rearrange("(h p) -> p h", p=P))
            small(gw[:], gate_w.rearrange("(k p) e -> p k e", p=P))
            sp.dma_start(xs, x_view[:, 0:TB, :]).then_inc(x_in, 16)
            with sp.Fori(1, NB) as b:
                sp.wait_ge(x_turned, b)
                sp.dma_start(xs, x_view[:, ds(b * TB, TB), :]).then_inc(x_in, 16)
            gu_view = wgu[:].rearrange("p (e k f) -> p e k f", e=E + 1, k=H)
            sp.dma_start(gu_view[:, E], ws_gu.rearrange("(k p) f -> p k f", p=P)).then_inc(shared_in, 16)
            sp.dma_start(wds[:].rearrange("p (k d) -> p k d", k=KF),
                         ws_dn.rearrange("(k p) d -> p k d", p=P)).then_inc(shared_in, 16)
            for e in range(E):
                sp.dma_start(gu_view[:, e], w_gu[e].rearrange("(k p) f -> p k f", p=P)).then_inc(gu_in, 16)
            sp.wait_ge(consts, 1)
            for i in range(SPARE):
                sp.dma_start(slots[E * REGION + i * P:E * REGION + (i + 1) * P, :],
                             zeros[:]).then_inc(spare_zeroed, 16)
            sp.wait_ge(y_added, NB * N)
            sp.wait_ge(v_ready, NB)
            dn_view = wdn.rearrange("p (e k d) -> p e k d", e=E, k=KF)
            for e in range(E):
                sp.dma_start(dn_view[:, e], w_dn[e].rearrange("(k p) d -> p k d", p=P)).then_inc(dn_in, 16)
            sp.wait_ge(table_ready, 1)
            for e in range(E):
                n = sp.value_load(cnti[0:1, e:e + 1], min_val=0, max_val=NT * P)
                sp.dma_start(slots[ds(n + e * REGION, P), :], zeros[:]).then_inc(zeroed, 16)
            sp.wait_ge(zeroed, 16 * E)
            sp.wait_ge(spare_zeroed, 16 * SPARE)
            sp.wait_ge(scattered, 16 * TOP * NT)

            def load(j, s):
                row = sp.value_load(tab_r[0:1, ds(j, 1)], min_val=0, max_val=ROWS - P)
                sp.dma_start(page_in[:, s, :], slots[ds(row, P), :]).then_inc(slot_in[s], 16)

            def store(j, s):
                sp.dma_start(slots_y[ds(j * P, P), :], yo[:, s, :]).then_inc(slot_out[s], 16)

            for j in range(PAGES):
                load(j, j)
            for j in range(PAGES):
                sp.wait_ge(page_turned, j + 1)
                load(j + PAGES, j)
                if j > 0:
                    sp.wait_ge(y_read, j)
                    store(j - 1, (j - 1) % 2)
            with sp.Fori(1, RT // PAGES - 1) as i:
                for s in range(PAGES):
                    sp.wait_ge(page_turned, i * PAGES + (s + 1))
                    load(i * PAGES + (PAGES + s), s)
                    sp.wait_ge(y_read, i * PAGES + s)
                    store(i * PAGES + (s - 1), (s - 1) % 2)
            for j in range(RT - PAGES - 1, RT):
                sp.wait_ge(y_read, j + 1)
                store(j, j % 2)

        @block.gpsimd
        def _(pool):
            step = Chain(pool, pool_steps)
            nc.gpsimd.memset(zeros[:], 0.0).then_inc(consts, 1)
            step.link(nc.gpsimd.memset(ident[:], 0.0))
            step.link(nc.gpsimd.affine_select(out=ident[:], in_=ident[:], compare_op=ALU.not_equal, fill=1.0,
                                              base=0, pattern=[[-1, P]], channel_multiplier=1))
            step.link(nc.gpsimd.memset(ones[:], 1.0))
            step.link(nc.gpsimd.affine_select(out=tri[:], in_=ones[:], compare_op=ALU.is_gt, fill=0.0,
                                              base=0, pattern=[[1, P]], channel_multiplier=-1))
            step.link(nc.gpsimd.memset(sel[:], 0.0))
            for i in range(PARTS):
                step.link(nc.gpsimd.affine_select(out=sel[:], in_=sel[:], compare_op=ALU.not_equal, fill=1.0,
                                                  base=-i * BC, pattern=[[-1, BC], [0, P]],
                                                  channel_multiplier=1))
            step.link(nc.gpsimd.iota(iota8[:], pattern=[[1, E]], base=0, channel_multiplier=0,
                                     allow_small_or_imprecise_dtypes=True))
            step.link(nc.gpsimd.iota(base8[:], pattern=[[REGION, E]], base=0, channel_multiplier=0,
                                     allow_small_or_imprecise_dtypes=True))
            step.link(nc.gpsimd.iota(jrow[:], pattern=[[1, RT]], base=0, channel_multiplier=0,
                                     allow_small_or_imprecise_dtypes=True))
            step.link(nc.gpsimd.iota(jbase[:], pattern=[[P, RT]], base=0, channel_multiplier=0,
                                     allow_small_or_imprecise_dtypes=True))
            step.link(nc.gpsimd.memset(cum[:], 0.0))
            nc.gpsimd.memset(onerow[:], 1.0).then_inc(consts, 1)

            def scan_batch(b, g0, first, last):
                for n in range(N):
                    if n in BY_POOL:
                        inject(pool, b, g0, n, first)
                    if not first and n == 11:
                        scatter(b)

            def scatter(b):
                pool.wait_ge(idx_ready, b)
                alone(pool)
                for j in range(TB):
                    for k in range(TOP):
                        pool.indirect_dma_start(
                            out=slots[:, :],
                            out_offset=bass.IndirectOffsetOnAxis(ap=idx_now[:, j * TOP + k:j * TOP + k + 1], axis=0),
                            in_=x1b[:, j, :], in_offset=None).then_inc(scattered, 16)

            pool.wait_ge(prep_done, NB)
            scan_batch(0, 0, True, False)
            with pool.Fori(1, NB - 1) as b:
                scan_batch(b, b * N, False, False)
            scan_batch(NB - 1, (NB - 1) * N, False, True)
            scatter(NB)
            pool.wait_ge(idx_ready, NB + 1)
            pool.wait_ge(slot_out[0], 16 * (RT // 2))
            pool.wait_ge(slot_out[1], 16 * (RT // 2))
            for t in range(NT):
                j = t % TB
                if t >= TB:
                    pool.wait_ge(v_final, t - TB + 1)
                for k in range(TOP):
                    pool.indirect_dma_start(
                        out=gat[:, j, k, :], out_offset=None, in_=slots_y[:, :],
                        in_offset=bass.IndirectOffsetOnAxis(ap=idx_all[:, t * TOP + k:t * TOP + k + 1], axis=0),
                    ).then_inc(gathered[j], 16)

        @block.tensor
        def _(pe):
            pe.wait_ge(small_in, 16 * 9)
            pe.wait_ge(consts, 2)
            for k in range(H):
                nc.tensor.transpose(bank[0][:, k * P:(k + 1) * P], wx[:, k * P:(k + 1) * P], ident[:])
                nc.tensor.transpose(bank[0][:, (2 + k) * P:(3 + k) * P], dtw[:, k, :], ident[:])
                last = nc.tensor.transpose(bank[1][:, k * P:k * P + PARTS * BC], wbc[:, k * P:(k + 1) * P],
                                           ident[0:PARTS * BC, 0:PARTS * BC])
            last.then_inc(wT_made, 1)
            pe.wait_ge(wT_ready, 2)

            def prepare(b, first):
                pe.wait_ge(x_in, b * 16 + 16)
                if not first:
                    pe.wait_ge(dr_made, b)
                for h in range(H):
                    for j in range(TB):
                        last = nc.tensor.transpose(bank[h][:, j * P:(j + 1) * P],
                                                   xs[:, j, h * P:(h + 1) * P], ident[:])
                last.then_inc(x_turned, 1)
                pe.wait_ge(xT_act, b + 1)
                pe.wait_ge(xT_dve, b + 1)
                if not first:
                    pe.wait_ge(dr_kept, b)
                for k in range(H):
                    last = nc.tensor.matmul(bank[2][:], wT[:, k * P:(k + 1) * P], xT[:, ds(b, 1), k, :].rearrange("p o l -> p (o l)"),
                                            start=k == 0, stop=k == H - 1)
                last.then_inc(dr_made, 1)
                if not first:
                    pe.wait_ge(bc_read, b)
                for k in range(H):
                    last = nc.tensor.matmul(bank[3][0:PARTS * BC, :], wbcT[:, k, :], xT[:, ds(b, 1), k, :].rearrange("p o l -> p (o l)"),
                                            start=k == 0, stop=k == H - 1)
                last.then_inc(bc_made, 1)
                pe.wait_ge(dr_kept, b + 1)
                if not first:
                    pe.wait_ge(prep_done, b)
                for h in range(H):
                    last = nc.tensor.matmul(bank[4 + h][:], wT[:, (2 + h) * P:(3 + h) * P], drT,
                                            start=True, stop=True)
                last.then_inc(z_made, 1)

            prepare(0, True)
            with pe.Fori(1, NB) as b:
                prepare(b, False)
            pe.wait_ge(prep_done, NB)

            def spread_B(b, g, n):
                if not isinstance(g, int) or g > 0:
                    pe.wait_ge(B_kept, g)
                nc.tensor.matmul(psB[:], sel[:, n, :], stack[:, ds(b * L, L)],
                                 start=True, stop=True).then_inc(B_ready, 1)

            def spread_C(b, g, n, first):
                if not (first and n < 2):
                    pe.wait_ge(hC_ready, g - 1)
                nc.tensor.matmul(psC[n % 2][:], sel[:, N + n, :], stack[:, ds(b * L, L)],
                                 start=True, stop=True).then_inc(C_ready, 1)

            def add_y(g, n):
                pe.wait_ge(hC_ready, g + 1)
                for h in range(H):
                    last = nc.tensor.matmul(psY[h][:], ident[:], hC[:, n % 2, h, :], start=n == 0, stop=n == N - 1)
                last.then_inc(y_added, 1)

            def turn_v(b):
                pe.wait_ge(v_ready, b)
                for j in range(TB):
                    for h in range(H):
                        last = nc.tensor.transpose(psT[j][:, h * P:(h + 1) * P], vb[:, h, j * P:(j + 1) * P], ident[:])
                last.then_inc(v_turned, 1)

            def turn_x(b):
                pe.wait_ge(x1_ready, b)
                for j in range(TB):
                    for k in range(H):
                        last = nc.tensor.transpose(psT[j][:, k * P:(k + 1) * P], x1b[:, j, k * P:(k + 1) * P], ident[:])
                last.then_inc(X_turned, 1)

            def logits(b, first):
                pe.wait_ge(XT_ready, b)
                if not first:
                    pe.wait_ge(add_done, b * TB - TB)
                for j in range(TB):
                    for k in range(H):
                        last = nc.tensor.matmul(psL[:, j * E:(j + 1) * E], xTb[:, j, k, :], gw[:, k, :],
                                                start=k == 0, stop=k == H - 1)
                last.then_inc(L_made, 1)

            def ranks(b, first):
                pe.wait_ge(mask_ready, b)
                if not first:
                    pe.wait_ge(cum_ready, b - 1)
                nc.tensor.matmul(psL, tri[:], mask[:].rearrange("p j e -> p (j e)"), start=True, stop=False)
                for j in range(TB):
                    rows = (cum[:] if j == 0 else mask[:, j - 1, :]).unsqueeze(1).to_broadcast([P, TB - j, E])
                    last = nc.tensor.matmul(psL[:, j * E:].rearrange("p (j e) -> p j e", e=E), ones[:], rows,
                                            start=False, stop=j == TB - 1)
                last.then_inc(rank_made, 1)

            def gate_or_up(e, c, x_of, done):
                for k in range(H):
                    last = nc.tensor.matmul((psG, psU)[c][:], x_of(k), gu(e, k, c), start=k == 0, stop=k == H - 1)
                last.then_inc(done, 1)

            def gate(u, e, x_of):
                if not isinstance(u, int) or u > 0:
                    pe.wait_ge(silu_done, u)
                gate_or_up(e, 0, x_of, G_made)

            def up(u, e, x_of):
                if not isinstance(u, int) or u > 0:
                    pe.wait_ge(hp_ready, u)
                gate_or_up(e, 1, x_of, U_made)

            def turn_h(u):
                pe.wait_ge(hp_ready, u + 1)
                for k in range(KF):
                    last = nc.tensor.transpose(psM[:, k * P:(k + 1) * P], hp[:, k * P:(k + 1) * P], ident[:])
                last.then_inc(H_turned, 1)

            def down(u, w, out):
                pe.wait_ge(hT_ready, u + 1)
                for k in range(KF):
                    last = nc.tensor.matmul(out, hT[:, k, :], w(k), start=k == 0, stop=k == KF - 1)
                last.then_inc(O_made, 1)

            def w_shared(k):
                return wds[:, k * D:(k + 1) * D]

            def shared_step(b, m, first):
                if m == 2:
                    turn_v(b)
                if m == 5:
                    turn_x(b)
                if m == 6:
                    logits(b, first)
                if m == 8:
                    ranks(b, first)
                for j in range(TB):
                    u = b * TB + (j - TB)
                    if m == 6 + 2 * j:
                        if j == 0:
                            pe.wait_ge(XT_ready, b)
                        gate(u, E, lambda k: xTb[:, j, k, :])
                    if m == 7 + 2 * j:
                        up(u, E, lambda k: xTb[:, j, k, :])
                    if m == 8 + 2 * j:
                        if j == 0:
                            pe.wait_ge(idx_ready, b)
                        else:
                            pe.wait_ge(add_done, u)
                        turn_h(u)
                    if m == 9 + 2 * j:
                        down(u, w_shared, psM[:, 0:D])

            def scan_batch(b, g0, first, last, second=False):
                if first:
                    spread_B(b, 0, 0)
                    spread_B(b, 1, 1)
                for m in range(N):
                    if m + 2 < N:
                        spread_B(b, g0 + (m + 2), m + 2)
                    elif not last:
                        spread_B(b + 1, g0 + (m + 2), m + 2 - N)
                    spread_C(b, g0 + m, m, first)
                    if m == 2 and not first:
                        pe.wait_ge(v_ready, b)
                    if m >= 2:
                        add_y(g0 + (m - 2), m - 2)
                    if not first:
                        shared_step(b, m, second)
                add_y(g0 + (N - 2), N - 2)
                add_y(g0 + (N - 1), N - 1)

            pe.wait_ge(shared_in, 32)
            scan_batch(0, 0, True, False)
            scan_batch(1, N, False, False, True)
            with pe.Fori(2, NB - 1) as b:
                scan_batch(b, b * N, False, False)
            scan_batch(NB - 1, (NB - 1) * N, False, True)
            for m in range(N):
                shared_step(NB, m, False)
            pe.wait_ge(cum_ready, NB)
            pe.wait_ge(add_done, NT)
            nc.tensor.matmul(psM[:, 0:E], ones[:], cum[:], start=True, stop=True).then_inc(count_made, 1)

            def expert_of(j):
                return pe.value_load(tab_e[0:1, ds(j, 1)], min_val=0, max_val=E - 1)

            def w_of(e):
                return lambda k: wdn[:, ds(e * (KF * D) + k * D, D)]

            def turn_page(j, s, fills):
                pe.wait_ge(slot_in[s % PAGES], fills * 16)
                if not isinstance(j, int) or j > 0:
                    pe.wait_ge(page_kept, j)
                for k in range(H):
                    last = nc.tensor.transpose(psX[:, k * P:(k + 1) * P], page_in[:, s % PAGES, k * P:(k + 1) * P],
                                               ident[:])
                last.then_inc(page_turned, 1)

            def routed_tile(j, s, before, fills, first=False, last=False):
                e = expert_of(j)
                pe.wait_ge(page_kept, j + 1)
                x_of = lambda k: xTs[:, s % 2, k, :]
                gate(j + NT, e, x_of)
                if not first:
                    turn_h(j + (NT - 1))
                if not last:
                    turn_page(j + 1, s + 1, fills)
                up(j + NT, e, x_of)
                if not first:
                    pe.wait_ge(y_read, j - 1) if not isinstance(j, int) or j > 1 else None
                    down(j + (NT - 1), w_of(before), psO[:, 0:D])
                return e

            pe.wait_ge(table_ready, 1)
            pe.wait_ge(gu_in, 16 * E)
            pe.wait_ge(dn_in, 16 * E)
            turn_page(0, 0, 1)
            e = None
            for j in range(PAGES):
                e = routed_tile(j, j, e, 1 + (j + 1) // PAGES, first=j == 0)
            with pe.Fori(1, RT // PAGES - 1) as i:
                e = expert_of(i * PAGES - 1)
                for s in range(PAGES):
                    e = routed_tile(i * PAGES + s, s, e, i + (1 + (s + 1) // PAGES))
            e = expert_of(RT - PAGES - 1)
            for j in range(RT - PAGES, RT):
                e = routed_tile(j, j % PAGES, e, (j + 1) // PAGES + 1, last=j == RT - 1)
            turn_h(NT + RT - 1)
            pe.wait_ge(y_read, RT - 1)
            down(NT + RT - 1, w_of(e), psO[:, 0:D])

        @block.scalar
        def _(act):
            step = Chain(act, s_steps)
            act.wait_ge(small_in, 16 * 9)
            nc.scalar.activation(aexp[:], alog[:], ACT.Exp).then_inc(a_exp, 1)
            def prepare(b, first):
                step.start(b * 2)
                act.wait_ge(x_turned, b + 1)
                alone(act)
                nc.scalar.activation(xT[:, ds(b, 1), 0, :].rearrange("p o l -> p (o l)"), bank[0][:], ACT.Copy).then_inc(xT_act, 1)
                act.wait_ge(dr_made, b + 1)
                if not first:
                    act.wait_ge(z_made, b)
                nc.scalar.activation(drT, bank[2][:], ACT.Copy).then_inc(dr_kept, 1)
                act.wait_ge(zb_ready, b + 1)
                if not first:
                    act.wait_ge(prep_done, b)
                step.link(nc.scalar.activation(ab, zb, ACT.Abs))
                step.link(nc.scalar.activation(ab, ab, ACT.Exp, scale=-1.0))
                nc.scalar.activation(ab, ab, ACT.Ln, bias=1.0).then_inc(ab_ready, 1)

            prepare(0, True)
            with act.Fori(1, NB) as b:
                prepare(b, False)
            act.wait_ge(a_ready, 1)
            act.wait_ge(prep_done, NB)

            def keep_B(b, g, n, first):
                act.wait_ge(B_ready, g + 1)
                dBu_made_before(act, b, n, RING, first)
                nc.scalar.activation(Bs[:, n % RING], psB[:], ACT.Copy).then_inc(B_kept, 1)

            def decays(b, g, n, first):
                if not (first and n < 2):
                    act.wait_ge(h_ready, g - 1)
                    alone(act)
                for h in range(H):
                    last = nc.scalar.activation(dA[:, n % 2, h, :],
                                                delta[:, ds(b, 1), h, :].rearrange("p o l -> p (o l)"), ACT.Exp,
                                                scale=aneg[:, h, n:n + 1])
                last.then_inc(dA_ready, 1)

            def inv_std(count):
                act.wait_ge(var_ready, count)
                step.link(nc.scalar.activation(lnv[:], ve[:], ACT.Ln))
                nc.scalar.activation(r0[:], lnv[:], ACT.Exp, scale=-0.5).then_inc(rstd_ready, 1)

            def keep_hT(u):
                act.wait_ge(H_turned, u + 1)
                if not isinstance(u, int) or u > 0:
                    act.wait_ge(O_made, u)
                nc.scalar.activation(hT[:].rearrange("p k m -> p (k m)"), psM[:], ACT.Copy).then_inc(hT_ready, 1)

            def shared_step(b, m, second):
                if m == 4:
                    inv_std(b)
                if m == 5:
                    act.wait_ge(X_turned, b)
                    if not second:
                        act.wait_ge(U_made, b * TB - TB)
                    for j in range(0, TB, 2):
                        last = nc.scalar.activation(xTb[:, j:j + 2].rearrange("p j k m -> p (j k m)"),
                                                    (psG, psU)[j // 2][:], ACT.Copy)
                    last.then_inc(XT_ready, 1)
                for j in range(TB):
                    u = b * TB + (j - TB)
                    if m == 6 + 2 * j:
                        act.wait_ge(G_made, u + 1)
                        if not isinstance(u, int) or u > 0:
                            act.wait_ge(hp_ready, u)
                        nc.scalar.activation(sg[:], psG[:], ACT.Tanh, scale=0.5).then_inc(tanh_done, 1)
                    if m == 8 + 2 * j:
                        keep_hT(u)

            def scan_batch(b, g0, first, last, second=False):
                step.start(b + (NB * 2 - 1) if not first else NB * 2)
                if first:
                    keep_B(b, 0, 0, True)
                    keep_B(b, 1, 1, True)
                for n in range(N):
                    decays(b, g0 + n, n, first)
                    if n + 2 < N:
                        keep_B(b, g0 + (n + 2), n + 2, first)
                    elif not last:
                        keep_B(b + 1, g0 + (n + 2), n + 2 - N, False)
                    if not first:
                        shared_step(b, n, second)

            scan_batch(0, 0, True, False)
            scan_batch(1, N, False, False, True)
            with act.Fori(2, NB - 1) as b:
                scan_batch(b, b * N, False, False)
            scan_batch(NB - 1, (NB - 1) * N, False, True)
            step.start(NB * 3 - 1)
            for m in range(N):
                shared_step(NB, m, False)

            def keep_page(j, s):
                act.wait_ge(page_turned, j + 1)
                if not isinstance(j, int) or j > 1:
                    act.wait_ge(U_made, j + (NT - 1))
                nc.scalar.activation(xTs[:, s % 2].rearrange("p k m -> p (k m)"), psX[:, 0:D],
                                     ACT.Copy).then_inc(page_kept, 1)

            def routed_tile(j, s, first=False, last=False):
                act.wait_ge(G_made, j + (NT + 1))
                act.wait_ge(hp_ready, j + NT)
                nc.scalar.activation(sg[:], psG[:], ACT.Silu).then_inc(silu_done, 1)
                if not first:
                    keep_hT(j + (NT - 1))
                if not last:
                    keep_page(j + 1, s + 1)

            keep_page(0, 0)
            for j in range(PAGES):
                routed_tile(j, j, first=j == 0)
            with act.Fori(1, RT // PAGES - 1) as i:
                for s in range(PAGES):
                    routed_tile(i * PAGES + s, s)
            for j in range(RT - PAGES, RT):
                routed_tile(j, j % PAGES, last=j == RT - 1)
            keep_hT(NT + RT - 1)
            act.wait_ge(idx_ready, NB)
            nc.scalar.activation(edif[:], dif[:], ACT.Exp).then_inc(edif_ready, 1)
            with act.Fori(0, NB) as b:
                step.start(b + NB * 3)
                inv_std(b + (NB + 1))
                act.wait_ge(out_ready, b + 1)
                act.dma_start(out_view[:, ds(b * TB, TB), :], ofin).then_inc(stored, 16)
            act.wait_ge(stored, 16 * NB)

        @block.vector
        def _(dve):
            step = Chain(dve, v_steps)
            V = nc.vector
            dve.wait_ge(small_in, 16 * 9)
            V.tensor_scalar(dsk1[:], dsk[:], 1.0, None, ALU.add)
            dve.wait_ge(a_exp, 1)
            V.tensor_scalar(aneg[:], aexp[:], -1.0, None, ALU.mult).then_inc(a_ready, 1)
            dve.wait_ge(wT_made, 1)
            V.tensor_copy(wT[:], bank[0][:]).then_inc(wT_ready, 1)
            V.tensor_copy(wbcT[:], bank[1][:, 0:H * P].rearrange("p (k m) -> p k m", k=H)[:, :, 0:PARTS * BC]
                          ).then_inc(wT_ready, 1)

            PREP = 5
            rest = vb[0:PARTS * BC, 0, :]
            with dve.Fori(0, NB) as b:
                step.start(b * PREP)
                dve.wait_ge(x_turned, b + 1)
                alone(dve)
                V.tensor_copy(xT[:, ds(b, 1), 1, :].rearrange("p o l -> p (o l)"), bank[1][:]).then_inc(xT_dve, 1)
                dve.wait_ge(bc_made, b + 1)
                step.link(V.tensor_copy(stack[:, ds(b * L, L)], bank[3][0:PARTS * BC, :]))
                step.link(V.tensor_tensor(rest, bank[3][0:PARTS * BC, :], stack[:, ds(b * L, L)], ALU.subtract), alone)
                for i in range(1, PARTS):
                    last = V.tensor_copy(stack[i * BC:(i + 1) * BC, ds(b * L, L)], vb[i * BC:(i + 1) * BC, 0, :])
                step.link(last)
                step.link(V.tensor_tensor(vb[2 * BC:3 * BC, 1, :], vb[2 * BC:3 * BC, 0, :],
                                          stack[2 * BC:3 * BC, ds(b * L, L)], ALU.subtract), alone)
                V.tensor_copy(stack[2 * BC:3 * BC, ds(b * L, L)], vb[2 * BC:3 * BC, 1, :]).then_inc(bc_read, 1)
                dve.wait_ge(z_made, b + 1)
                for h in range(H):
                    last = V.tensor_scalar(zb[:, h, :], bank[4 + h][:], dtb[:, h:h + 1], None, ALU.add)
                last.then_inc(zb_ready, 1)
                dve.wait_ge(zb_ready, b + 1)
                dve.wait_ge(ab_ready, b + 1)
                step.link(V.scalar_tensor_tensor(delta[:, ds(b, 1)].rearrange("p o h l -> p (o h) l"), zb, 0.0, ab, ALU.max, ALU.add))
                dve.wait_ge(xT_act, b + 1)
                V.tensor_tensor(du[:, ds(b, 1)].rearrange("p o h l -> p (o h) l"), delta[:, ds(b, 1)].rearrange("p o h l -> p (o h) l"), xT[:, ds(b, 1)].rearrange("p o h l -> p (o h) l"),
                                ALU.mult).then_inc(prep_done, 1)

            def scan(b, g, n, first):
                dBu_made(dve, b, n)
                dve.wait_ge(dA_ready, g + 1)
                if not (first and n < 2):
                    dve.wait_ge(hC_ready, g - 1)
                for h in range(H):
                    last = V.tensor_tensor_scan(hs[:, n % 2, h, :], dA[:, n % 2, h, :], dBu[:, n % RING, h, :], 0.0,
                                                ALU.mult, ALU.add)
                last.then_inc(h_ready, 1)

            def project(g, n, first):
                dve.wait_ge(h_ready, g + 1)
                dve.wait_ge(C_ready, g + 1)
                if not (first and n < 2):
                    dve.wait_ge(y_added, g - 1)
                V.tensor_tensor(hC[:, n % 2], hs[:, n % 2], psC[n % 2][:].unsqueeze(1).to_broadcast([P, H, L]),
                                ALU.mult).then_inc(hC_ready, 1)

            def residual(b, second):
                dve.wait_ge(y_added, b * N)
                if not second:
                    dve.wait_ge(scattered, b * (16 * TOP * TB) - 16 * TOP * TB)
                    dve.wait_ge(add_done, b * TB - TB)
                for h in range(H):
                    last = V.scalar_tensor_tensor(vb[:, h, :], xT[:, ds(b - 1, 1), h, :].rearrange("p o l -> p (o l)"),
                                                  dsk1[:, h:h + 1], psY[h][:], ALU.mult, ALU.add)
                last.then_inc(v_ready, 1)

            def inv_std(count):
                dve.wait_ge(rstd_ready, count)
                step.link(V.tensor_tensor(r1[:], r0[:], r0[:], ALU.mult))
                step.link(V.tensor_tensor(r2[:], r1[:], ve[:], ALU.mult))
                step.link(V.tensor_scalar(r3[:], r2[:], -0.5, 1.5, ALU.mult, ALU.add))
                step.link(V.tensor_tensor(rstd[:], r0[:], r3[:], ALU.mult))

            def stats(tiles):
                for j, tile in enumerate(tiles):
                    last = V.bn_stats(st6[:, j, :], tile)
                step.link(last, alone)
                for j in range(TB):
                    last = V.bn_aggr(mv[:, j, :], st6[:, j, :])
                step.link(last)
                V.tensor_scalar(ve[:], mv[:, :, 1], EPS, None, ALU.add).then_inc(var_ready, 1)

            def norm(b):
                inv_std(b)
                for j in range(TB):
                    last = V.tensor_scalar(x1b[:, j, :], psT[j], mv[:, j, 0:1], rstd[:, j:j + 1],
                                           ALU.subtract, ALU.mult)
                last.then_inc(x1_ready, 1)

            def choose(b):
                dve.wait_ge(L_made, b)
                step.link(V.tensor_copy(lg[:].rearrange("p j e -> p (j e)"), psL), alone)
                for j in range(TB):
                    last = V.max(mx8[:, j, :], lg[:, j, :])
                step.link(last, alone)
                for j in range(TB):
                    last = V.max_index(ix8[:, j, :], mx8[:, j, :], lg[:, j, :])
                V.tensor_tensor(dif[:, ds(b * TB - TB, TB)], mx8[:, :, 1], mx8[:, :, 0], ALU.subtract)
                step.link(last)
                step.link(V.tensor_copy(ixf[:], ix8[:, :, 0:TOP]))
                picks = ixf[:].rearrange("p j k -> p (j k)")
                V.tensor_scalar(ex_all[:, ds(b * TB * TOP - TB * TOP, TB * TOP)], picks, 0.0, None, ALU.add)
                step.link(V.tensor_tensor(oh[:], picks.unsqueeze(2).to_broadcast([P, TB * TOP, E]),
                                          iota8[:].unsqueeze(1).to_broadcast([P, TB * TOP, E]), ALU.is_equal))
                both_k = oh[:].rearrange("p (j k) e -> p j k e", k=TOP)
                V.tensor_tensor(mask[:], both_k[:, :, 0, :], both_k[:, :, 1, :], ALU.add).then_inc(mask_ready, 1)

            def place(b):
                dve.wait_ge(mask_ready, b)
                step.link(V.tensor_reduce(new8[:], mask[:].rearrange("p j e -> p e j"), AX.X, ALU.add))
                dve.wait_ge(rank_made, b)
                V.tensor_tensor(cum[:], cum[:], new8[:], ALU.add).then_inc(cum_ready, 1)
                step.link(V.tensor_tensor(rank8[:], psL.rearrange("p (j e) -> p j e", e=E),
                                          base8[:].unsqueeze(1).to_broadcast([P, TB, E]), ALU.add))
                both_k = oh[:].rearrange("p (j k) e -> p j k e", k=TOP)
                picks = pick[:].rearrange("p (j k) e -> p j k e", k=TOP)
                for k in range(TOP):
                    last = V.tensor_tensor(picks[:, :, k, :], both_k[:, :, k, :], rank8[:], ALU.mult)
                step.link(last)
                step.link(V.tensor_reduce(slotf[:], pick[:], AX.X, ALU.add))
                V.tensor_scalar(slot_all[:, ds(b * TB * TOP - TB * TOP, TB * TOP)], slotf[:], 0.0, None, ALU.add)
                V.tensor_copy(idx_now[:], slotf[:]).then_inc(idx_ready, 1)

            def shared_product(u):
                dve.wait_ge(tanh_done, u + 1)
                dve.wait_ge(G_made, u + 1)
                V.scalar_tensor_tensor(sg[:], sg[:], 1.0, psG[:], ALU.add, ALU.mult).then_inc(silu_done, 1)
                dve.wait_ge(silu_done, u + 1)
                dve.wait_ge(U_made, u + 1)
                if not isinstance(u, int) or u > 0:
                    dve.wait_ge(H_turned, u)
                V.scalar_tensor_tensor(hp[:], sg[:], 0.5, psU[:], ALU.mult, ALU.mult).then_inc(hp_ready, 1)

            def add_shared(u, j):
                dve.wait_ge(O_made, u + 1)
                V.tensor_tensor(total[:, ds(u, 1), :].rearrange("p o d -> p (o d)"), x1b[:, j, :], psM[:, 0:D],
                                ALU.add).then_inc(add_done, 1)

            def shared_step(b, m, second):
                if m == 1:
                    residual(b, second)
                if m == 3:
                    dve.wait_ge(v_turned, b)
                    alone(dve)
                    stats(psT)
                if m == 4:
                    norm(b)
                if m == 6:
                    choose(b)
                if m == 8:
                    place(b)
                for j in range(TB):
                    u = b * TB + (j - TB)
                    if m == 7 + 2 * j:
                        shared_product(u)
                    if m == 9 + 2 * j:
                        add_shared(u, j)

            SCAN = 15

            def scan_batch(b, g0, first, last, second=False):
                for n in range(N):
                    if n not in BY_POOL:
                        inject(dve, b, g0, n, first)
                    if n >= 1:
                        project(g0 + (n - 1), n - 1, first)
                    elif not first:
                        project(g0 - 1, N - 1, False)
                    scan(b, g0 + n, n, first)
                    if not first:
                        shared_step(b, n, second)
                if last:
                    project(g0 + (N - 1), N - 1, False)

            step.start(NB * PREP)
            scan_batch(0, 0, True, False)
            scan_batch(1, N, False, False, True)
            with dve.Fori(2, NB - 1) as b:
                step.start(b * SCAN + (NB * PREP - SCAN))
                scan_batch(b, b * N, False, False)
            step.start((NB - 2) * SCAN + NB * PREP)
            scan_batch(NB - 1, (NB - 1) * N, False, True)
            for m in range(N):
                shared_step(NB, m, False)
            scanned = NB * (PREP + SCAN)
            step.start(scanned)
            dve.wait_ge(count_made, 1)
            step.link(V.tensor_copy(cnt[:], psM[:, 0:E]))
            step.link(V.tensor_copy(cnti[:], cnt[:]))
            step.link(V.tensor_scalar(pgi[:], cnt[:], float(P - 1), None, ALU.add))
            step.link(V.tensor_single_scalar(pgs[:], pgi[:], P.bit_length() - 1, ALU.arith_shift_right))
            step.link(V.tensor_copy(pages[:], pgs[:]))
            step.link(V.tensor_tensor_scan(ends[:], onerow[:], pages[:], 0.0, ALU.mult, ALU.add))
            step.link(V.tensor_scalar(skip[:], pages[:], -float(P), float(REGION), ALU.mult, ALU.add))
            step.link(V.tensor_tensor(past, jrow[:].unsqueeze(2).to_broadcast([1, RT, E]),
                                      ends[0:1, :].unsqueeze(1).to_broadcast([1, RT, E]), ALU.is_ge))
            step.link(V.tensor_tensor(jump, past, skip[0:1, :].unsqueeze(1).to_broadcast([1, RT, E]), ALU.mult))
            step.link(V.tensor_reduce(esum[:], past, AX.X, ALU.add))
            step.link(V.tensor_reduce(rsum[:], jump, AX.X, ALU.add))
            step.link(V.tensor_tensor(rowf[:], rsum[:], jbase[:], ALU.add))
            step.link(V.tensor_copy(tab_r[:], rowf[:]))
            V.tensor_scalar(tab_e[:], esum[:], float(E - 1), None, ALU.min).then_inc(table_ready, 1)
            step.link(V.tensor_tensor(starts[:], ends[:], pages[:], ALU.subtract))
            step.link(V.scalar_tensor_tensor(shift[:], starts[:], -float(P), base8[:], ALU.mult, ALU.add))
            step.link(V.tensor_tensor(is_ex, ex_all[:].unsqueeze(2).to_broadcast([P, NT * TOP, E]),
                                      iota8[:].unsqueeze(1).to_broadcast([P, NT * TOP, E]), ALU.is_equal))
            step.link(V.tensor_tensor(moved, is_ex, shift[:].unsqueeze(1).to_broadcast([P, NT * TOP, E]),
                                      ALU.mult))
            step.link(V.tensor_reduce(back[:], moved, AX.X, ALU.add))
            step.link(V.tensor_tensor(row_y[:], slot_all[:], back[:], ALU.subtract))
            V.tensor_copy(idx_all[:], row_y[:]).then_inc(idx_ready, 1)

            def keep_y(j, s, stores):
                dve.wait_ge(O_made, j + (NT + 1))
                if stores is not None:
                    dve.wait_ge(slot_out[s % 2], stores * 16)
                V.tensor_copy(yo[:, s % 2, :], psO[:, 0:D]).then_inc(y_read, 1)

            def routed_tile(j, s, stores):
                dve.wait_ge(silu_done, j + (NT + 1))
                dve.wait_ge(U_made, j + (NT + 1))
                dve.wait_ge(H_turned, j + NT)
                V.tensor_tensor(hp[:], sg[:], psU[:], ALU.mult).then_inc(hp_ready, 1)
                if not isinstance(j, int) or j > 0:
                    keep_y(j - 1, s + 1, stores)

            for j in range(PAGES):
                routed_tile(j, j, (j - 1) // 2 if j > 2 else None)
            with dve.Fori(1, RT // PAGES) as i:
                for s in range(PAGES):
                    routed_tile(i * PAGES + s, s, i * 2 + (s - 1) // 2)
            keep_y(RT - 1, RT - 1, RT // 2 - 1)
            dve.wait_ge(edif_ready, 1)
            step.link(V.tensor_scalar(eden[:], edif[:], 1.0, None, ALU.add))
            step.link(V.reciprocal(wt0[:], eden[:]))
            step.link(V.tensor_tensor(wt1[:], wt0[:], edif[:], ALU.mult))
            head = scanned + step.n

            FIN = 1 + 6

            def finish(b, first):
                step.start(b * FIN + head)
                for j in range(TB):
                    dve.wait_ge(gathered[j], b * (16 * TOP) + 16 * TOP)
                    row = total[:, ds(b * TB + j, 1), :].rearrange("p o d -> p (o d)")
                    last = V.scalar_tensor_tensor(row, gat[:, j, 0, :], wt0[:, ds(b * TB + j, 1)], row,
                                                  ALU.mult, ALU.add)
                step.link(last)
                for j in range(TB):
                    row = total[:, ds(b * TB + j, 1), :].rearrange("p o d -> p (o d)")
                    V.scalar_tensor_tensor(vfin[:, j, :], gat[:, j, 1, :], wt1[:, ds(b * TB + j, 1)], row,
                                           ALU.mult, ALU.add).then_inc(v_final, 1)
                dve.wait_ge(v_final, b * TB + TB)
                alone(dve)
                stats([vfin[:, j, :] for j in range(TB)])
                inv_std(b + (NB + 1))
                if not first:
                    dve.wait_ge(stored, b * 16)
                for j in range(TB):
                    last = V.tensor_scalar(ofin[:, j, :], vfin[:, j, :], mv[:, j, 0:1], rstd[:, j:j + 1],
                                           ALU.subtract, ALU.mult)
                last.then_inc(out_ready, 1)

            finish(0, True)
            with dve.Fori(1, NB) as b:
                finish(b, False)


_INS = ["L0_attn_x", "L0_attn_A_log", "L0_attn_D", "L0_attn_x_proj_w", "L0_attn_dt_proj_w", "L0_attn_dt_proj_b",
        "L0_ffn_gate_w", "L0_ffn_w_gate_up", "L0_ffn_w_down", "L0_ffn_shared_gate_up", "L0_ffn_shared_down"]


def kernel(**inputs):
    import numpy as _np
    import concourse.bacc as _bacc
    from concourse import mybir as _mybir
    from concourse.bass_utils import run_bass_kernel_spmd as _run

    nc = _bacc.Bacc("TRN2", target_bir_lowering=False, num_devices=1)
    arrays, args = {}, []
    for name in _INS:
        a = _np.ascontiguousarray(inputs[name])
        arrays[f"in_{name}"] = a
        args.append(nc.dram_tensor(f"in_{name}", a.shape, _mybir.dt.from_np(a.dtype), kind="ExternalInput").ap())
    out = nc.dram_tensor("out_0", inputs["L0_attn_x"].shape, _mybir.dt.float32, kind="ExternalOutput").ap()
    mamba_moe(nc, *args, out)
    r = _run(nc, [arrays], core_ids=[0])
    return r.results[0]["out_0"]
```

```python
from contextlib import ExitStack

import concourse.bass as bass
from concourse import mybir

ALU = mybir.AluOpType
ACT = mybir.ActivationFunctionType
F32 = mybir.dt.float32
BF16 = mybir.dt.bfloat16
I32 = mybir.dt.int32
U32 = mybir.dt.uint32
AX = mybir.AxisListType
ds = bass.ds

BY_VECTOR = (12, 15)
V_KEEP, STATS, NORM, X_TURN = 1, 3, 4, 5
LOGITS, CHOOSE, WEIGH, RANKS, PLACE = 6, 6, 7, 8, 8
SCATTER = 11
FIRST_GATE = 8
RESIDUAL = 14
GATE, UP, PRODUCT, H_TURN, DOWN, ADD = 0, 1, 2, 2, 3, 4
P = 128
EPS = 1e-5


class Chain:

    def __init__(self, engine, sem):
        self.engine, self.sem, self.base, self.n = engine, sem, 0, 0

    def link(self, instruction, alone=None):
        self.n += 1
        instruction.then_inc(self.sem, 1)
        self.engine.wait_ge(self.sem, self.base + self.n)
        if alone:
            alone(self.engine)

    def start(self, base):
        self.base, self.n = base, 0


def mamba_moe(nc, x, a_log, d_skip, x_proj_w, dt_w, dt_b, gate_w, w_gu, w_dn, ws_gu, ws_dn, out):
    NB, L, D = x.shape
    N = a_log.shape[1]
    R = dt_w.shape[1]
    E, _, F2 = w_gu.shape
    F = F2 // 2
    H = D // P
    NT = NB * L // P
    TB = L // P
    KF = F // P
    TOP = 2
    PAGES = 4
    BC = 2 * N
    PARTS = 3
    RT = (NT * P * TOP + E * (P - 1)) // P
    LOOPED = (RT - 1) // PAGES
    REGION = NT * P + P
    SPARE = RT - NT * TOP
    ROWS = E * REGION + SPARE * P
    W = D + 4
    ID, W1, DW, E0 = D, D + 1, D + 2, D + 3
    assert H == 2 and R == P and L == 512 and F == 512 and E == 8 and N == 16

    slots = nc.dram_tensor("slots_x", (ROWS, W), F32, kind="Internal").ap()
    sums = nc.dram_tensor("sums", (NT * P + P, D), F32, kind="Internal").ap()
    x_view = x.rearrange("b (j p) d -> p (b j) d", p=P)
    out_view = out.rearrange("b (j p) d -> p (b j) d", p=P)
    sums_view = sums[0:NT * P, :].rearrange("(t p) d -> p t d", p=P)

    with ExitStack() as ctx:
        def sb(name, shape, dt=F32):
            return ctx.enter_context(nc.sbuf_tensor(name, shape, dt))

        def sem(name):
            return ctx.enter_context(nc.semaphore(name))

        wgu = sb("wgu", [P, (E + 1) * H * F2])
        wds = sb("wds", [P, KF * D])
        both = sb("both", [P, NB * H * L])
        xT = both[:].rearrange("p (b h l) -> p b h l", b=NB, h=H)
        total = both[:].rearrange("p (t d) -> p t d", d=D)
        stack = sb("stack", [PARTS * BC, NB * L], BF16)
        sel = sb("sel", [PARTS * BC, BC, P], BF16)
        vx = sb("vx", [P, TB * W])
        x1b = vx[:].rearrange("p (j d) -> p j d", j=TB)
        rest = vx[0:PARTS * BC, 0:2 * L].rearrange("p (s l) -> p s l", s=2)
        xTb = sb("xTb", [P, TB, H, P])
        sg = sb("sg", [P, F])
        hp = sb("hp", [P, F])
        hT = sb("hT", [P, KF, P])
        ident = sb("ident", [P, P])
        tri = sb("tri", [P, P], BF16)
        ones = sb("ones", [P, P], BF16)
        zeros = sb("zeros", [P, W])
        wT = sb("wT", [P, 4 * P])
        wbcT = sb("wbcT", [P, H, PARTS * BC])
        alog = sb("alog", [P, H, N])
        aexp = sb("aexp", [P, H, N])
        aneg = sb("aneg", [P, H, N])
        dsk = sb("dsk", [P, H])
        dsk1 = sb("dsk1", [P, H])
        dtb = sb("dtb", [P, H])
        gw = sb("gw", [P, H, E])
        st6 = sb("st6", [P, TB, 6])
        mv = sb("mv", [P, TB, 2])
        ve = sb("ve", [P, TB])
        lnv = sb("lnv", [P, TB])
        r0 = sb("r0", [P, TB])
        r1 = sb("r1", [P, TB])
        r2 = sb("r2", [P, TB])
        r3 = sb("r3", [P, TB])
        rstd = sb("rstd", [P, TB])
        iota8 = sb("iota8", [P, E])
        base8 = sb("base8", [P, E])
        lg = sb("lg", [P, TB, E])
        mx8 = sb("mx8", [P, TB, 8])
        ix8 = sb("ix8", [P, TB, 8], U32)
        ixf = sb("ixf", [P, TB, TOP])
        oh = sb("oh", [P, TB * TOP, E])
        mask = sb("mask", [P, TB, E], BF16)
        cum = sb("cum", [P, E], BF16)
        new8 = sb("new8", [P, E])
        rank8 = sb("rank8", [P, TB, E])
        pick = sb("pick", [P, TB * TOP, E])
        slotf = sb("slotf", [P, TB * TOP])
        ids = sb("ids", [P, NT])
        idx_now = sb("idx_now", [P, TB * TOP], U32)
        dif = sb("dif", [P, TB])
        edif = sb("edif", [P, TB])
        eden = sb("eden", [P, TB])
        wt0 = sb("wt0", [P, TB])
        cnt = sb("cnt", [P, E])
        cnti = sb("cnti", [P, E], I32)
        pgi = sb("pgi", [P, E], I32)
        pgs = sb("pgs", [P, E], I32)
        pages = sb("pages", [P, E])
        onerow = sb("onerow", [P, E])
        ends = sb("ends", [P, E])
        skip = sb("skip", [P, E])
        row_page = sb("row_page", [P, PAGES], U32)
        jrow = sb("jrow", [P, RT])
        jbase = sb("jbase", [1, RT])
        esum = sb("esum", [P, RT])
        rsum = sb("rsum", [1, RT])
        rowf = sb("rowf", [1, RT])
        tab_e = sb("tab_e", [1, RT], I32)
        tab_r = sb("tab_r", [1, RT], I32)

        RING = 4
        ROOM = 2 * H * L * 3 + RING * (H + 1) * L + 2 * H * NB * L
        arena = sb("arena", [P, ROOM])
        at = [0]

        def room(n):
            at[0] += n
            assert at[0] <= ROOM
            return arena[:, at[0] - n:at[0]]

        dA = room(2 * H * L).rearrange("p (s h l) -> p s h l", s=2, h=H)
        dBu = room(RING * H * L).rearrange("p (s h l) -> p s h l", s=RING, h=H)
        Bs = room(RING * L).rearrange("p (s l) -> p s l", s=RING)
        h_at = at[0]
        hs = room(2 * H * L).rearrange("p (s h l) -> p s h l", s=2, h=H)
        hC = room(2 * H * L).rearrange("p (s h l) -> p s h l", s=2, h=H)
        xd = wgu[:, (E - 1) * H * F2:(E - 1) * H * F2 + H * L].rearrange("p (h l) -> p h l", h=H)
        delta = room(NB * H * L).rearrange("p (b h l) -> p b h l", b=NB, h=H)
        du = room(NB * H * L).rearrange("p (b h l) -> p b h l", b=NB, h=H)
        at[0] = 0
        wx = room(D)
        wbc = room(D)[0:PARTS * BC, :]
        dtw = room(H * R).rearrange("p (h r) -> p h r", h=H)
        at[0] = h_at
        xs = room(TB * D).rearrange("p (j d) -> p j d", j=TB)
        drT = room(L)
        at[0] = 0
        wdn = room(E * KF * D)
        page_in = room(PAGES * W).rearrange("p (s d) -> p s d", s=PAGES)
        xTs = room(2 * D).rearrange("p (s k m) -> p s k m", s=2, k=H)
        yo = room(2 * D).rearrange("p (s d) -> p s d", s=2)
        vfin = room(NT * D).rearrange("p (t d) -> p t d", d=D)
        HT = NT // 2
        BY_ACT = 3
        st6_fin = room(NT * 6).rearrange("p (t c) -> p t c", c=6)
        mv_fin = room(NT * 2).rearrange("p (t c) -> p t c", c=2)
        ve_fin, ln_fin, r0_fin, sq_fin, vr_fin, r3_fin, rstd_fin, shift_fin = [room(NT) for _ in range(8)]
        w_match = room(PAGES)
        w_page = room(PAGES)
        past = room(RT * E).rearrange("p (t e) -> p t e", e=E)
        jump = room(RT * E)[0:1, :].rearrange("p (t e) -> p t e", e=E)

        bank = [ctx.enter_context(nc.psum_tensor(f"bank{i}", [P, 512], F32)) for i in range(8)]
        psB, psC, psY, psG, psU, psM = bank[0], bank[1:3], bank[3:5], bank[5], bank[6], bank[7]
        psL = psM[:, 0:TB * E]
        psT = [(psG, psU)[j // 2][:, (j % 2) * D:(j % 2 + 1) * D] for j in range(TB)]
        psX = bank[0]
        psO = bank[1]
        psT_last = [bank[j // 2][:, (j % 2) * D:(j % 2 + 1) * D] for j in range(TB)]
        psN = bank[2][:, 0:E]

        proj_in = sem("proj_in")
        small_in = sem("small_in")
        x_in = sem("x_in")
        shared_in = sem("shared_in")
        gu_in = sem("gu_in")
        last_gu_in = sem("last_gu_in")
        dn_in = sem("dn_in")
        consts = sem("consts")
        ident_made = sem("ident_made")
        pool_steps = sem("pool_steps")
        wT_made = sem("wT_made")
        wT_ready = sem("wT_ready")
        a_exp = sem("a_exp")
        a_ready = sem("a_ready")
        x_turned = sem("x_turned")
        xT_ready = sem("xT_ready")
        dr_made = sem("dr_made")
        bc_made = sem("bc_made")
        dr_kept = sem("dr_kept")
        bc_read = sem("bc_read")
        z_made = sem("z_made")
        zb_ready = sem("zb_ready")
        ab_ready = sem("ab_ready")
        delta_ready = sem("delta_ready")
        du_ready = sem("du_ready")
        v_steps = sem("v_steps")
        s_steps = sem("s_steps")
        B_ready = sem("B_ready")
        C_ready = sem("C_ready")
        dBu_ready = sem("dBu_ready")
        dA_ready = sem("dA_ready")
        h_ready = sem("h_ready")
        hC_ready = sem("hC_ready")
        y_added = sem("y_added")
        xd_ready = sem("xd_ready")
        v_made = sem("v_made")
        v_kept = sem("v_kept")
        var_ready = sem("var_ready")
        rstd_ready = sem("rstd_ready")
        x1_ready = sem("x1_ready")
        x1_kept = sem("x1_kept")
        B_kept = sem("B_kept")
        pool_dBu = sem("pool_dBu")
        X_turned = sem("X_turned")
        XT_ready = sem("XT_ready")
        L_made = sem("L_made")
        G_made = sem("G_made")
        U_made = sem("U_made")
        tanh_done = sem("tanh_done")
        silu_done = sem("silu_done")
        hp_ready = sem("hp_ready")
        H_turned = sem("H_turned")
        hT_ready = sem("hT_ready")
        O_made = sem("O_made")
        mask_ready = sem("mask_ready")
        rank_made = sem("rank_made")
        idx_ready = sem("idx_ready")
        scattered = sem("scattered")
        count_made = sem("count_made")
        counted = sem("counted")
        table_ready = sem("table_ready")
        zeroed = sem("zeroed")
        spare_zeroed = sem("spare_zeroed")
        slot_in = [sem(f"slot_in{i}") for i in range(PAGES)]
        page_turned = sem("page_turned")
        page_kept = sem("page_kept")
        y_read = sem("y_read")
        add_done = sem("add_done")
        cum_ready = sem("cum_ready")
        dif_ready = sem("dif_ready")
        edif_ready = sem("edif_ready")
        meta_read = sem("meta_read")
        sums_begun = sem("sums_begun")
        last_begun = sem("last_begun")
        added = sem("added")
        final_in = [sem(f"final_in{b}") for b in range(NB)]
        ve_ready = sem("ve_ready")
        root_ready = sem("root_ready")
        scale_ready = sem("scale_ready")
        out_act = sem("out_act")
        out_ready = sem("out_ready")
        stored = sem("stored")
        passed = {nc.scalar: sem("passed_act"), nc.vector: sem("passed_dve"), nc.gpsimd: sem("passed_pool")}

        PAIRS = N // 2

        def alone(engine):
            engine.sem_inc(passed[engine], 1)

        block = ctx.enter_context(nc.Block())

        def gu(e, k, c):
            if isinstance(e, int):
                a = (e * H + k) * F2 + c * F
                return wgu[:, a:a + F]
            return wgu[:, ds(e * (H * F2) + (k * F2 + c * F), F)]

        def channels(b, h):
            return xT[:, ds(b, 1), h, :].rearrange("p o l -> p (o l)")

        def of_batch(buffer, b):
            return buffer[:, ds(b, 1)].rearrange("p o h l -> p (o h) l")

        def tiles_at(b, m, part, second):
            found = []
            for j in range(TB):
                at = FIRST_GATE + 3 * j + part
                if at == m:
                    found.append((b * TB + (j - TB), j, b))
                elif at == m + N and not second:
                    found.append((b * TB + (j - 2 * TB), j, b - 1))
            return found

        def done_in_scan(part):
            return FIRST_GATE + 3 * (TB - 2) + part < N

        BY_POOL = [n for n in range(N) if n not in BY_VECTOR]
        NP, NV = len(BY_POOL), N - len(BY_POOL)

        def dBu_made(engine, b, n):
            before = sum(m in BY_POOL for m in range(n))
            if n in BY_POOL:
                engine.wait_ge(pool_dBu, b * NP + (before + 1))
            else:
                engine.wait_ge(dBu_ready, b * NV + (n - before + 1))

        def dBu_made_before(engine, b, n, back, first):
            if n >= back:
                dBu_made(engine, b, n - back)
            elif not first:
                dBu_made(engine, b - 1, n - back + N)

        def inject(engine, b, g0, n, first):
            engine.wait_ge(B_kept, g0 + (n + 1))
            if not (first and n < RING):
                engine.wait_ge(h_ready, g0 + (n - (RING - 1)))
            if n in BY_POOL:
                alone(engine)
            engine.tensor_tensor(dBu[:, n % RING], du[:, ds(b, 1)].rearrange("p o h l -> p (o h) l"),
                                 Bs[:, n % RING].unsqueeze(1).to_broadcast([P, H, L]),
                                 ALU.mult).then_inc(pool_dBu if n in BY_POOL else dBu_ready, 1)

        @block.sync
        def _(sp):
            def small(dst, src):
                sp.dma_start(dst, src).then_inc(proj_in, 16)

            small(wx, x_proj_w[0:R, :])
            for i in range(PARTS):
                small(wbc[i * BC:(i + 1) * BC, :], x_proj_w[R:R + BC, :])
            small(dtw, dt_w.rearrange("(h p) r -> p h r", p=P))
            sp.dma_start(xs, x_view[:, 0:TB, :]).then_inc(x_in, 16)
            with sp.Fori(1, NB) as b:
                sp.wait_ge(x_turned, b)
                sp.dma_start(xs, x_view[:, ds(b * TB, TB), :]).then_inc(x_in, 16)
            gu_view = wgu[:].rearrange("p (e k f) -> p e k f", e=E + 1, k=H)
            sp.dma_start(gu_view[:, E], ws_gu.rearrange("(k p) f -> p k f", p=P)).then_inc(shared_in, 16)
            sp.dma_start(wds[:].rearrange("p (k d) -> p k d", k=KF),
                         ws_dn.rearrange("(k p) d -> p k d", p=P)).then_inc(shared_in, 16)
            for e in range(E - 1):
                sp.dma_start(gu_view[:, e], w_gu[e].rearrange("(k p) f -> p k f", p=P)).then_inc(gu_in, 16)
            sp.wait_ge(consts, 1)
            for i in range(SPARE):
                sp.dma_start(slots[E * REGION + i * P:E * REGION + (i + 1) * P, :],
                             zeros[:]).then_inc(spare_zeroed, 16)
            sp.dma_start(sums[NT * P:NT * P + P, :], zeros[:, 0:D]).then_inc(sums_begun, 16)
            with sp.Fori(0, NB - 1) as b:
                sp.wait_ge(add_done, b * TB + TB)
                sp.dma_start(sums_view[:, ds(b * TB, TB), :], total[:, ds(b * TB, TB), :]).then_inc(sums_begun, 16)
            sp.wait_ge(v_made, NB)
            sp.dma_start(gu_view[:, E - 1], w_gu[E - 1].rearrange("(k p) f -> p k f", p=P)).then_inc(last_gu_in, 16)
            dn_view = wdn.rearrange("p (e k d) -> p e k d", e=E, k=KF)
            for e in range(E):
                sp.dma_start(dn_view[:, e], w_dn[e].rearrange("(k p) d -> p k d", p=P)).then_inc(dn_in, 16)
            sp.wait_ge(counted, 1)
            for e in range(E):
                n = sp.value_load(cnti[0:1, e:e + 1], min_val=0, max_val=NT * P)
                sp.dma_start(slots[ds(n + e * REGION, P), :], zeros[:]).then_inc(zeroed, 16)
            sp.wait_ge(zeroed, 16 * E)
            sp.wait_ge(spare_zeroed, 16 * SPARE)
            sp.wait_ge(scattered, 16 * TOP * NT)
            sp.wait_ge(table_ready, 1)

            def load(j, s):
                row = sp.value_load(tab_r[0:1, ds(j, 1)], min_val=0, max_val=ROWS - P)
                sp.dma_start(page_in[:, s, :], slots[ds(row, P), :]).then_inc(slot_in[s], 16)

            for j in range(PAGES):
                load(j, j)

            def load_after(j, s):
                sp.wait_ge(page_turned, j - (PAGES - 1))
                sp.wait_ge(meta_read, j - (PAGES - 1))
                load(j, s)

            with sp.Fori(1, LOOPED) as i:
                for s in range(PAGES):
                    load_after(i * PAGES + s, s)
            for j in range(LOOPED * PAGES, RT):
                load_after(j, j % PAGES)
            sp.wait_ge(added, 16 * RT)
            for b in range(NB):
                sp.dma_start(vfin[:, b * TB:(b + 1) * TB, :], sums_view[:, b * TB:(b + 1) * TB, :]
                             ).then_inc(final_in[b], 16)
            for half in range(2):
                t = half * HT
                sp.wait_ge(out_ready, half + 1)
                sp.dma_start(out_view[:, t + BY_ACT:t + HT, :], vfin[:, t + BY_ACT:t + HT, :]).then_inc(stored, 16)
                sp.wait_ge(out_act, half + 1)
                sp.dma_start(out_view[:, t:t + BY_ACT, :], vfin[:, t:t + BY_ACT, :]).then_inc(stored, 16)
            sp.wait_ge(stored, 16 * 4)

        @block.gpsimd
        def _(pool):
            step = Chain(pool, pool_steps)
            step.link(nc.gpsimd.memset(zeros[:], 0.0))
            nc.gpsimd.iota(zeros[:, ID:ID + 1], pattern=[[0, 1]], base=NT * P, channel_multiplier=1,
                           allow_small_or_imprecise_dtypes=True).then_inc(consts, 1)
            step.link(nc.gpsimd.memset(ident[:], 0.0))
            step.link(nc.gpsimd.affine_select(out=ident[:], in_=ident[:], compare_op=ALU.not_equal, fill=1.0,
                                              base=0, pattern=[[-1, P]], channel_multiplier=1))
            pool.sem_inc(ident_made, 1)
            step.link(nc.gpsimd.memset(ones[:], 1.0))
            step.link(nc.gpsimd.affine_select(out=tri[:], in_=ones[:], compare_op=ALU.is_gt, fill=0.0,
                                              base=0, pattern=[[1, P]], channel_multiplier=-1))
            step.link(nc.gpsimd.iota(iota8[:], pattern=[[1, E]], base=0, channel_multiplier=0,
                                     allow_small_or_imprecise_dtypes=True))
            step.link(nc.gpsimd.iota(base8[:], pattern=[[REGION, E]], base=0, channel_multiplier=0,
                                     allow_small_or_imprecise_dtypes=True))
            step.link(nc.gpsimd.iota(jrow[:], pattern=[[1, RT]], base=0, channel_multiplier=0,
                                     allow_small_or_imprecise_dtypes=True))
            step.link(nc.gpsimd.iota(ids[:], pattern=[[P, NT]], base=0, channel_multiplier=1,
                                     allow_small_or_imprecise_dtypes=True))
            step.link(nc.gpsimd.iota(jbase[:], pattern=[[P, RT]], base=0, channel_multiplier=0,
                                     allow_small_or_imprecise_dtypes=True))
            step.link(nc.gpsimd.memset(cum[:], 0.0))
            step.link(nc.gpsimd.memset(onerow[:], 1.0))
            step.link(nc.gpsimd.memset(sel[:], 0.0))
            for i in range(PARTS):
                last = nc.gpsimd.affine_select(out=sel[:], in_=sel[:], compare_op=ALU.not_equal, fill=1.0,
                                               base=-i * BC, pattern=[[-1, BC], [0, P]],
                                               channel_multiplier=1)
                if i < PARTS - 1:
                    step.link(last)
            last.then_inc(consts, 1)

            def scan_batch(b, g0, first, last):
                for n in range(N):
                    if n in BY_POOL:
                        inject(pool, b, g0, n, first)
                    if not first and SCATTER <= n < SCATTER + TB:
                        scatter(b, n - SCATTER)
                    if first and n == 4:
                        times_x(NB - 2)
                    if first and n == 10:
                        times_x(NB - 1)

            def scatter(b, j):
                if j == 0:
                    pool.wait_ge(idx_ready, b)
                    alone(pool)
                for k in range(TOP):
                    pool.indirect_dma_start(
                        out=slots[:, :],
                        out_offset=bass.IndirectOffsetOnAxis(ap=idx_now[:, j * TOP + k:j * TOP + k + 1], axis=0),
                        in_=x1b[:, j, :], in_offset=None).then_inc(scattered, 16)

            def times_x(b):
                pool.wait_ge(delta_ready, b + 1)
                pool.wait_ge(xT_ready, b + 1)
                alone(pool)
                pool.tensor_tensor(of_batch(du, b), of_batch(delta, b), of_batch(xT, b), ALU.mult).then_inc(du_ready, 1)

            with pool.Fori(0, NB - 2) as b:
                times_x(b)
            pool.wait_ge(du_ready, 1)
            scan_batch(0, 0, True, False)
            pool.wait_ge(du_ready, NB)
            with pool.Fori(1, NB - 1) as b:
                scan_batch(b, b * N, False, False)
            scan_batch(NB - 1, (NB - 1) * N, False, True)
            for j in range(TB):
                scatter(NB, j)
            pool.wait_ge(add_done, NT)
            pool.dma_start(sums_view[:, NT - TB:NT, :], total[:, NT - TB:NT, :]).then_inc(last_begun, 16)

            def add_page(j, s):
                pool.wait_ge(y_read, j + 1)
                if not isinstance(j, int) or j > 0:
                    pool.wait_ge(added, j * 16)
                alone(pool)
                pool.indirect_dma_start(
                    out=sums[:, :], out_offset=bass.IndirectOffsetOnAxis(ap=row_page[:, s:s + 1], axis=0),
                    in_=yo[:, s % 2, :], in_offset=None, compute_op=ALU.add).then_inc(added, 16)

            pool.wait_ge(sums_begun, 16 * NB)
            pool.wait_ge(last_begun, 16)
            for j in range(PAGES):
                add_page(j, j)
            with pool.Fori(1, LOOPED) as i:
                for s in range(PAGES):
                    add_page(i * PAGES + s, s)
            for j in range(LOOPED * PAGES, RT):
                add_page(j, j % PAGES)

        @block.tensor
        def _(pe):
            pe.wait_ge(proj_in, 16 * 5)
            pe.wait_ge(ident_made, 1)
            for k in range(H):
                nc.tensor.transpose(bank[5][:, k * P:(k + 1) * P], wx[:, k * P:(k + 1) * P], ident[:])
                nc.tensor.transpose(bank[5][:, (2 + k) * P:(3 + k) * P], dtw[:, k, :], ident[:])
                last = nc.tensor.transpose(bank[6][:, k * P:k * P + PARTS * BC], wbc[:, k * P:(k + 1) * P],
                                           ident[0:PARTS * BC, 0:PARTS * BC])
            last.then_inc(wT_made, 1)

            def turn(b, first):
                pe.wait_ge(x_in, b * 16 + 16)
                if not first:
                    pe.wait_ge(xT_ready, b)
                for h in range(H):
                    for j in range(TB):
                        last = nc.tensor.transpose(bank[h][:, j * P:(j + 1) * P],
                                                   xs[:, j, h * P:(h + 1) * P], ident[:])
                last.then_inc(x_turned, 1)

            def project(b, first):
                pe.wait_ge(xT_ready, b + 1)
                if not first:
                    pe.wait_ge(dr_kept, b)
                for k in range(H):
                    last = nc.tensor.matmul(bank[2][:], wT[:, k * P:(k + 1) * P], channels(b, k),
                                            start=k == 0, stop=k == H - 1)
                last.then_inc(dr_made, 1)
                if not first:
                    pe.wait_ge(bc_read, b)
                for k in range(H):
                    last = nc.tensor.matmul(bank[3][0:PARTS * BC, :], wbcT[:, k, :], channels(b, k),
                                            start=k == 0, stop=k == H - 1)
                last.then_inc(bc_made, 1)

            def project_delta(b, first):
                pe.wait_ge(dr_kept, b + 1)
                if not first:
                    pe.wait_ge(zb_ready, b)
                for h in range(H):
                    last = nc.tensor.matmul(bank[4 + h][:], wT[:, (2 + h) * P:(3 + h) * P], drT,
                                            start=True, stop=True)
                last.then_inc(z_made, 1)

            turn(0, True)
            pe.wait_ge(wT_ready, 2)
            project(0, True)
            turn(1, False)
            project_delta(0, True)
            turn(2, False)
            project(1, False)
            with pe.Fori(1, NB - 2) as b:
                project_delta(b, False)
                turn(b + 2, False)
                project(b + 1, False)
            project_delta(NB - 2, False)
            project(NB - 1, False)
            project_delta(NB - 1, False)
            pe.wait_ge(zb_ready, NB)
            pe.wait_ge(bc_read, NB)
            pe.wait_ge(consts, 2)

            def spread_B(b, g, n):
                if not isinstance(g, int) or g > 0:
                    pe.wait_ge(B_kept, g)
                nc.tensor.matmul(psB[:], sel[:, n, :], stack[:, ds(b * L, L)],
                                 start=True, stop=True).then_inc(B_ready, 1)

            def spread_C(b, g, n, first):
                if not (first and n < 2):
                    pe.wait_ge(hC_ready, g - 1)
                nc.tensor.matmul(psC[n % 2][:], sel[:, N + n, :], stack[:, ds(b * L, L)],
                                 start=True, stop=True).then_inc(C_ready, 1)

            def turn_onto(source, first, last):
                for j in range(TB):
                    for h in range(H):
                        out = psY[j // 2][:, (j % 2) * D + h * P:(j % 2) * D + (h + 1) * P]
                        ins = nc.tensor.matmul(out, source[:, h, j * P:(j + 1) * P], ident[:],
                                               start=first and j % 2 == 0 and h == 0,
                                               stop=last and j % 2 == 1 and h == H - 1,
                                               is_transpose=True, skip_group_check=True)
                return ins

            def add_y(g, n):
                pe.wait_ge(hC_ready, g + 1)
                turn_onto(hC[:, n % 2], n == 0, False).then_inc(y_added, 1)

            def add_x(b):
                pe.wait_ge(xd_ready, b + 1)
                turn_onto(xd, False, True).then_inc(v_made, 1)

            def turn_x(b, psT):
                pe.wait_ge(x1_ready, b)
                for j in range(TB):
                    for k in range(H):
                        last = nc.tensor.transpose(psT[j][:, k * P:(k + 1) * P], x1b[:, j, k * P:(k + 1) * P], ident[:])
                last.then_inc(X_turned, 1)

            def logits(b, first):
                if first:
                    pe.wait_ge(small_in, 16 * 4)
                pe.wait_ge(XT_ready, b)
                if not first:
                    pe.wait_ge(add_done, b * TB - TB)
                for j in range(TB):
                    for k in range(H):
                        last = nc.tensor.matmul(psL[:, j * E:(j + 1) * E], xTb[:, j, k, :], gw[:, k, :],
                                                start=k == 0, stop=k == H - 1)
                last.then_inc(L_made, 1)

            def ranks(b, first):
                pe.wait_ge(mask_ready, b)
                if not first:
                    pe.wait_ge(cum_ready, b - 1)
                nc.tensor.matmul(psL, tri[:], mask[:].rearrange("p j e -> p (j e)"), start=True, stop=False)
                for j in range(TB):
                    rows = (cum[:] if j == 0 else mask[:, j - 1, :]).unsqueeze(1).to_broadcast([P, TB - j, E])
                    last = nc.tensor.matmul(psL[:, j * E:].rearrange("p (j e) -> p j e", e=E), ones[:], rows,
                                            start=False, stop=j == TB - 1)
                last.then_inc(rank_made, 1)

            def gate_or_up(e, c, x_of, done):
                for k in range(H):
                    last = nc.tensor.matmul((psG, psU)[c][:], x_of(k), gu(e, k, c), start=k == 0, stop=k == H - 1)
                last.then_inc(done, 1)

            def gate(u, e, x_of):
                if not isinstance(u, int) or u > 0:
                    pe.wait_ge(silu_done, u)
                gate_or_up(e, 0, x_of, G_made)

            def up(u, e, x_of):
                if not isinstance(u, int) or u > 0:
                    pe.wait_ge(hp_ready, u)
                gate_or_up(e, 1, x_of, U_made)

            def turn_h(u):
                pe.wait_ge(hp_ready, u + 1)
                for k in range(KF):
                    last = nc.tensor.transpose(psM[:, k * P:(k + 1) * P], hp[:, k * P:(k + 1) * P], ident[:])
                last.then_inc(H_turned, 1)

            def down(u, w, out):
                pe.wait_ge(hT_ready, u + 1)
                for k in range(KF):
                    last = nc.tensor.matmul(out, hT[:, k, :], w(k), start=k == 0, stop=k == KF - 1)
                last.then_inc(O_made, 1)

            def w_shared(k):
                return wds[:, k * D:(k + 1) * D]

            x_of_tile = [lambda k, j=j: xTb[:, j, k, :] for j in range(TB)]

            def shared_step(b, m, second):
                if m == X_TURN:
                    if not second:
                        pe.wait_ge(hp_ready, b * TB - TB)
                    turn_x(b, psT)
                if m == LOGITS:
                    logits(b, second)
                if m == RANKS:
                    ranks(b, second)
                for u, j, _ in tiles_at(b, m, GATE, second):
                    if j == 0:
                        pe.wait_ge(XT_ready, b)
                    gate(u, E, x_of_tile[j])
                for u, j, _ in tiles_at(b, m, UP, second):
                    up(u, E, x_of_tile[j])
                for u, j, of in tiles_at(b, m, H_TURN, second):
                    if j == 0:
                        pe.wait_ge(idx_ready, of)
                    else:
                        pe.wait_ge(add_done, u)
                    turn_h(u)
                for u, j, _ in tiles_at(b, m, DOWN, second):
                    down(u, w_shared, psM[:, 0:D])

            def scan_batch(b, g0, first, last, second=False):
                if first:
                    spread_B(b, 0, 0)
                    spread_B(b, 1, 1)
                for m in range(N):
                    if m + 2 < N:
                        spread_B(b, g0 + (m + 2), m + 2)
                    elif not last:
                        spread_B(b + 1, g0 + (m + 2), m + 2 - N)
                    spread_C(b, g0 + m, m, first)
                    if m == 2 and not first:
                        pe.wait_ge(v_kept, b)
                    if m >= 2:
                        add_y(g0 + (m - 2), m - 2)
                    if not first:
                        shared_step(b, m, second)
                add_y(g0 + (N - 2), N - 2)
                add_y(g0 + (N - 1), N - 1)
                add_x(b)

            pe.wait_ge(shared_in, 32)
            scan_batch(0, 0, True, False)
            scan_batch(1, N, False, False, True)
            with pe.Fori(2, NB - 1) as b:
                scan_batch(b, b * N, False, False)
            scan_batch(NB - 1, (NB - 1) * N, False, True)
            left = NT - TB - 2
            if not done_in_scan(H_TURN):
                pe.wait_ge(add_done, left)
                turn_h(left)
            gate(left + 1, E, x_of_tile[TB - 1])
            down(left, w_shared, psM[:, 0:D])
            up(left + 1, E, x_of_tile[TB - 1])
            pe.wait_ge(add_done, left + 1)
            turn_h(left + 1)
            down(left + 1, w_shared, psM[:, 0:D])
            turn_x(NB, psT_last)
            logits(NB, False)
            gate(NT - TB, E, x_of_tile[0])
            ranks(NB, False)
            up(NT - TB, E, x_of_tile[0])
            pe.wait_ge(cum_ready, NB)
            nc.tensor.matmul(psN, ones[:], cum[:], start=True, stop=True).then_inc(count_made, 1)
            for j in range(TB):
                u = NT - TB + j
                if j == 0:
                    pe.wait_ge(idx_ready, NB)
                if j + 1 < TB:
                    gate(u + 1, E, x_of_tile[j + 1])
                if j > 0:
                    pe.wait_ge(add_done, u)
                turn_h(u)
                if j + 1 < TB:
                    up(u + 1, E, x_of_tile[j + 1])
                down(u, w_shared, psM[:, 0:D])

            def expert_of(j):
                return pe.value_load(tab_e[0:1, ds(j, 1)], min_val=0, max_val=E - 1)

            def w_of(e):
                return lambda k: wdn[:, ds(e * (KF * D) + k * D, D)]

            def turn_page(j, s, fills):
                pe.wait_ge(slot_in[s % PAGES], fills * 16)
                if not isinstance(j, int) or j > 0:
                    pe.wait_ge(page_kept, j)
                for k in range(H):
                    last = nc.tensor.transpose(psX[:, k * P:(k + 1) * P], page_in[:, s % PAGES, k * P:(k + 1) * P],
                                               ident[:])
                last.then_inc(page_turned, 1)

            def routed_tile(j, s, before, fills, first=False, last=False):
                e = expert_of(j)
                pe.wait_ge(page_kept, j + 1)
                x_of = lambda k: xTs[:, s % 2, k, :]
                gate(j + NT, e, x_of)
                if not first:
                    turn_h(j + (NT - 1))
                if not last:
                    turn_page(j + 1, s + 1, fills)
                up(j + NT, e, x_of)
                if not first:
                    pe.wait_ge(y_read, j - 1) if not isinstance(j, int) or j > 1 else None
                    down(j + (NT - 1), w_of(before), psO[:, 0:D])
                return e

            pe.wait_ge(table_ready, 1)
            pe.wait_ge(gu_in, 16 * (E - 1))
            pe.wait_ge(last_gu_in, 16)
            pe.wait_ge(dn_in, 16 * E)
            turn_page(0, 0, 1)
            e = None
            for j in range(PAGES):
                e = routed_tile(j, j, e, 1 + (j + 1) // PAGES, first=j == 0)
            with pe.Fori(1, LOOPED) as i:
                e = expert_of(i * PAGES - 1)
                for s in range(PAGES):
                    e = routed_tile(i * PAGES + s, s, e, i + (1 + (s + 1) // PAGES))
            e = expert_of(LOOPED * PAGES - 1)
            for j in range(LOOPED * PAGES, RT):
                e = routed_tile(j, j % PAGES, e, (j + 1) // PAGES + 1, last=j == RT - 1)
            turn_h(NT + RT - 1)
            pe.wait_ge(y_read, RT - 1)
            down(NT + RT - 1, w_of(e), psO[:, 0:D])

        @block.scalar
        def _(act):
            step = Chain(act, s_steps)

            def small(dst, src):
                act.dma_start(dst, src).then_inc(small_in, 16)

            small(alog[:], a_log.rearrange("(h p) n -> p h n", p=P))
            with nc.allow_non_contiguous_dma(reason="two columns of 128 scalars"):
                small(dsk[:], d_skip.rearrange("(h p) -> p h", p=P))
                small(dtb[:], dt_b.rearrange("(h p) -> p h", p=P))
            small(gw[:], gate_w.rearrange("(k p) e -> p k e", p=P))
            act.wait_ge(small_in, 16 * 4)
            nc.scalar.activation(aexp[:], alog[:], ACT.Exp).then_inc(a_exp, 1)
            def keep_dr(b, first):
                act.wait_ge(dr_made, b + 1)
                if not first:
                    act.wait_ge(z_made, b)
                nc.scalar.activation(drT, bank[2][:], ACT.Copy).then_inc(dr_kept, 1)

            def softplus(b):
                step.start(b * 2)
                act.wait_ge(zb_ready, b + 1)
                alone(act)
                step.link(nc.scalar.activation(of_batch(du, b), of_batch(delta, b), ACT.Abs), alone)
                step.link(nc.scalar.activation(of_batch(du, b), of_batch(du, b), ACT.Exp, scale=-1.0), alone)
                nc.scalar.activation(of_batch(du, b), of_batch(du, b), ACT.Ln, bias=1.0).then_inc(ab_ready, 1)

            keep_dr(0, True)
            with act.Fori(0, NB - 1) as b:
                keep_dr(b + 1, False)
                softplus(b)
            act.wait_ge(a_ready, 1)
            act.wait_ge(delta_ready, 1)

            def keep_B(b, g, n, first):
                act.wait_ge(B_ready, g + 1)
                dBu_made_before(act, b, n, RING, first)
                nc.scalar.activation(Bs[:, n % RING], psB[:], ACT.Copy).then_inc(B_kept, 1)

            def decays(b, g, n, first):
                if not (first and n < 2):
                    act.wait_ge(h_ready, g - 1)
                    alone(act)
                for h in range(H):
                    last = nc.scalar.activation(dA[:, n % 2, h, :],
                                                delta[:, ds(b, 1), h, :].rearrange("p o l -> p (o l)"), ACT.Exp,
                                                scale=aneg[:, h, n:n + 1])
                last.then_inc(dA_ready, 1)

            def inv_std(count):
                act.wait_ge(var_ready, count)
                step.link(nc.scalar.activation(lnv[:], ve[:], ACT.Ln))
                nc.scalar.activation(r0[:], lnv[:], ACT.Exp, scale=-0.5).then_inc(rstd_ready, 1)

            def keep_hT(u):
                act.wait_ge(H_turned, u + 1)
                if not isinstance(u, int) or u > 0:
                    act.wait_ge(O_made, u)
                nc.scalar.activation(hT[:].rearrange("p k m -> p (k m)"), psM[:], ACT.Copy).then_inc(hT_ready, 1)

            def keep_xTb(b, banks, second):
                act.wait_ge(X_turned, b)
                if not second:
                    act.wait_ge(U_made, b * TB - TB)
                for j in range(0, TB, 2):
                    last = nc.scalar.activation(xTb[:, j:j + 2].rearrange("p j k m -> p (j k m)"),
                                                banks[j // 2][:], ACT.Copy)
                last.then_inc(XT_ready, 1)

            def keep_x1(b):
                act.wait_ge(x1_ready, b)
                nc.scalar.activation(total[:, ds(b * TB - TB, TB), :], x1b[:, :, 0:D], ACT.Copy).then_inc(x1_kept, 1)

            def exp_dif(b):
                act.wait_ge(dif_ready, b)
                nc.scalar.activation(edif[:], dif[:], ACT.Exp).then_inc(edif_ready, 1)

            def tanh_gate(u):
                act.wait_ge(G_made, u + 1)
                if not isinstance(u, int) or u > 0:
                    act.wait_ge(hp_ready, u)
                nc.scalar.activation(sg[:], psG[:], ACT.Tanh, scale=0.5).then_inc(tanh_done, 1)

            def residual(b, first):
                if not first:
                    act.wait_ge(v_made, b)
                    alone(act)
                for h in range(H):
                    last = nc.scalar.activation(xd[:, h, :], channels(b, h), ACT.Copy, scale=dsk1[:, h:h + 1])
                last.then_inc(xd_ready, 1)

            def keep_v(b, second):
                act.wait_ge(v_made, b)
                if not second:
                    act.wait_ge(scattered, b * (16 * TOP * TB) - 16 * TOP * TB)
                    act.wait_ge(x1_kept, b - 1)
                for j in range(0, TB, 2):
                    last = nc.scalar.activation(x1b[:, j:j + 2, 0:D], psY[j // 2][:].rearrange("p (j d) -> p j d", j=2),
                                                ACT.Copy)
                last.then_inc(v_kept, 1)

            def shared_step(b, m, second):
                if m == V_KEEP:
                    keep_v(b, second)
                if m == NORM:
                    inv_std(b)
                if m == X_TURN:
                    keep_xTb(b, (psG, psU), second)
                if m == X_TURN:
                    keep_x1(b)
                if m == WEIGH:
                    exp_dif(b)
                for u, j, _ in tiles_at(b, m, GATE, second):
                    tanh_gate(u)
                for u, j, _ in tiles_at(b, m, H_TURN, second):
                    keep_hT(u)

            def scan_batch(b, g0, first, last, second=False):
                step.start(b + (NB * 2 - 1) if not first else NB * 2)
                if first:
                    keep_B(b, 0, 0, True)
                    keep_B(b, 1, 1, True)
                for n in range(N):
                    decays(b, g0 + n, n, first)
                    if n + 2 < N:
                        keep_B(b, g0 + (n + 2), n + 2, first)
                    elif not last:
                        keep_B(b + 1, g0 + (n + 2), n + 2 - N, False)
                    if first and n == 7:
                        softplus(NB - 1)
                    if n == RESIDUAL:
                        residual(b, first)
                    if not first:
                        shared_step(b, n, second)

            scan_batch(0, 0, True, False)
            act.wait_ge(delta_ready, NB)
            scan_batch(1, N, False, False, True)
            with act.Fori(2, NB - 1) as b:
                scan_batch(b, b * N, False, False)
            scan_batch(NB - 1, (NB - 1) * N, False, True)
            step.start(NB * 3 - 1)
            left = NT - TB - 2
            keep_v(NB, False)
            if not done_in_scan(H_TURN):
                keep_hT(left)
            tanh_gate(left + 1)
            inv_std(NB)
            keep_hT(left + 1)
            keep_xTb(NB, bank[0:2], False)
            keep_x1(NB)
            exp_dif(NB)
            for j in range(TB):
                tanh_gate(NT - TB + j)
                keep_hT(NT - TB + j)

            def keep_page(j, s):
                act.wait_ge(page_turned, j + 1)
                if not isinstance(j, int) or j > 1:
                    act.wait_ge(U_made, j + (NT - 1))
                nc.scalar.activation(xTs[:, s % 2].rearrange("p k m -> p (k m)"), psX[:, 0:D],
                                     ACT.Copy).then_inc(page_kept, 1)

            def routed_tile(j, s, first=False, last=False):
                act.wait_ge(G_made, j + (NT + 1))
                act.wait_ge(hp_ready, j + NT)
                nc.scalar.activation(sg[:], psG[:], ACT.Silu).then_inc(silu_done, 1)
                if not first:
                    keep_hT(j + (NT - 1))
                if not last:
                    keep_page(j + 1, s + 1)

            keep_page(0, 0)
            for j in range(PAGES):
                routed_tile(j, j, first=j == 0)
            with act.Fori(1, LOOPED) as i:
                for s in range(PAGES):
                    routed_tile(i * PAGES + s, s)
            for j in range(LOOPED * PAGES, RT):
                routed_tile(j, j % PAGES, last=j == RT - 1)
            keep_hT(NT + RT - 1)
            step.start(NB * 3)
            for half in range(2):
                t = half * HT
                act.wait_ge(ve_ready, half + 1)
                step.link(nc.scalar.activation(ln_fin[:, t:t + HT], ve_fin[:, t:t + HT], ACT.Ln))
                nc.scalar.activation(r0_fin[:, t:t + HT], ln_fin[:, t:t + HT], ACT.Exp,
                                     scale=-0.5).then_inc(root_ready, 1)
            for half in range(2):
                act.wait_ge(scale_ready, half + 1)
                for t in range(half * HT, half * HT + BY_ACT):
                    last = nc.scalar.activation(vfin[:, t, :], vfin[:, t, :], ACT.Identity,
                                                bias=shift_fin[:, t:t + 1], scale=rstd_fin[:, t:t + 1])
                last.then_inc(out_act, 1)

        @block.vector
        def _(dve):
            step = Chain(dve, v_steps)
            V = nc.vector
            dve.wait_ge(small_in, 16 * 4)
            V.tensor_scalar(dsk1[:], dsk[:], 1.0, None, ALU.add)
            dve.wait_ge(a_exp, 1)
            V.tensor_scalar(aneg[:], aexp[:], -1.0, None, ALU.mult).then_inc(a_ready, 1)
            dve.wait_ge(wT_made, 1)
            V.tensor_copy(wT[:], bank[5][:]).then_inc(wT_ready, 1)
            V.tensor_copy(wbcT[:], bank[6][:, 0:H * P].rearrange("p (k m) -> p k m", k=H)[:, :, 0:PARTS * BC]
                          ).then_inc(wT_ready, 1)

            PREP = 4

            def keep_x(b):
                dve.wait_ge(x_turned, b + 1)
                alone(dve)
                for h in range(H):
                    last = V.tensor_copy(channels(b, h), bank[h][:])
                last.then_inc(xT_ready, 1)

            def split(b):
                dve.wait_ge(bc_made, b + 1)
                step.link(V.tensor_copy(stack[:, ds(b * L, L)], bank[3][0:PARTS * BC, :]))
                step.link(V.tensor_tensor(rest[:, 0, :], bank[3][0:PARTS * BC, :], stack[:, ds(b * L, L)],
                                          ALU.subtract), alone)
                for i in range(1, PARTS):
                    last = V.tensor_copy(stack[i * BC:(i + 1) * BC, ds(b * L, L)], rest[i * BC:(i + 1) * BC, 0, :])
                step.link(last)
                step.link(V.tensor_tensor(rest[2 * BC:3 * BC, 1, :], rest[2 * BC:3 * BC, 0, :],
                                          stack[2 * BC:3 * BC, ds(b * L, L)], ALU.subtract), alone)
                V.tensor_copy(stack[2 * BC:3 * BC, ds(b * L, L)], rest[2 * BC:3 * BC, 1, :]).then_inc(bc_read, 1)

            def add_bias(b):
                dve.wait_ge(z_made, b + 1)
                for h in range(H):
                    last = V.tensor_scalar(delta[:, ds(b, 1), h, :].rearrange("p o l -> p (o l)"), bank[4 + h][:],
                                           dtb[:, h:h + 1], None, ALU.add)
                last.then_inc(zb_ready, 1)

            def finish_delta(b):
                dve.wait_ge(zb_ready, b + 1)
                dve.wait_ge(ab_ready, b + 1)
                alone(dve)
                V.scalar_tensor_tensor(of_batch(delta, b), of_batch(delta, b), 0.0, of_batch(du, b),
                                       ALU.max, ALU.add).then_inc(delta_ready, 1)

            keep_x(0)
            split(0)
            keep_x(1)
            add_bias(0)
            keep_x(2)
            step.start(PREP)
            split(1)
            with dve.Fori(1, NB - 2) as b:
                step.start(b * PREP + PREP)
                add_bias(b)
                finish_delta(b - 1)
                keep_x(b + 2)
                split(b + 1)
            step.start(NB * PREP - PREP)
            add_bias(NB - 2)
            finish_delta(NB - 3)
            split(NB - 1)
            add_bias(NB - 1)
            finish_delta(NB - 2)
            dve.wait_ge(du_ready, 1)

            def scan(b, g, n, first):
                dBu_made(dve, b, n)
                dve.wait_ge(dA_ready, g + 1)
                if not (first and n < 2):
                    dve.wait_ge(hC_ready, g - 1)
                for h in range(H):
                    last = V.tensor_tensor_scan(hs[:, n % 2, h, :], dA[:, n % 2, h, :], dBu[:, n % RING, h, :], 0.0,
                                                ALU.mult, ALU.add)
                last.then_inc(h_ready, 1)

            def project(g, n, first):
                dve.wait_ge(h_ready, g + 1)
                dve.wait_ge(C_ready, g + 1)
                if not (first and n < 2):
                    dve.wait_ge(y_added, g - 1)
                V.tensor_tensor(hC[:, n % 2], hs[:, n % 2], psC[n % 2][:].unsqueeze(1).to_broadcast([P, H, L]),
                                ALU.mult).then_inc(hC_ready, 1)

            def inv_std(count):
                dve.wait_ge(rstd_ready, count)
                step.link(V.tensor_tensor(r1[:], r0[:], r0[:], ALU.mult))
                step.link(V.tensor_tensor(r2[:], r1[:], ve[:], ALU.mult))
                step.link(V.tensor_scalar(r3[:], r2[:], -0.5, 1.5, ALU.mult, ALU.add))
                step.link(V.tensor_tensor(rstd[:], r0[:], r3[:], ALU.mult))

            def stats(tiles):
                for j, tile in enumerate(tiles):
                    last = V.bn_stats(st6[:, j, :], tile)
                step.link(last, alone)
                for j in range(TB):
                    last = V.bn_aggr(mv[:, j, :], st6[:, j, :])
                step.link(last)
                V.tensor_scalar(ve[:], mv[:, :, 1], EPS, None, ALU.add).then_inc(var_ready, 1)

            def norm(b):
                inv_std(b)
                for j in range(TB):
                    last = V.tensor_scalar(x1b[:, j, 0:D], x1b[:, j, 0:D], mv[:, j, 0:1], rstd[:, j:j + 1],
                                           ALU.subtract, ALU.mult)
                last.then_inc(x1_ready, 1)

            def choose(b):
                dve.wait_ge(L_made, b)
                step.link(V.tensor_copy(lg[:].rearrange("p j e -> p (j e)"), psL), alone)
                for j in range(TB):
                    last = V.max(mx8[:, j, :], lg[:, j, :])
                step.link(last, alone)
                for j in range(TB):
                    last = V.max_index(ix8[:, j, :], mx8[:, j, :], lg[:, j, :])
                V.tensor_tensor(dif[:], mx8[:, :, 1], mx8[:, :, 0], ALU.subtract).then_inc(dif_ready, 1)
                step.link(last)
                step.link(V.tensor_copy(ixf[:], ix8[:, :, 0:TOP]))
                picks = ixf[:].rearrange("p j k -> p (j k)")
                step.link(V.tensor_tensor(oh[:], picks.unsqueeze(2).to_broadcast([P, TB * TOP, E]),
                                          iota8[:].unsqueeze(1).to_broadcast([P, TB * TOP, E]), ALU.is_equal))
                both_k = oh[:].rearrange("p (j k) e -> p j k e", k=TOP)
                V.tensor_tensor(mask[:], both_k[:, :, 0, :], both_k[:, :, 1, :], ALU.add).then_inc(mask_ready, 1)

            def weigh(b):
                dve.wait_ge(edif_ready, b)
                V.tensor_scalar(x1b[:, :, ID], ids[:, ds(b * TB - TB, TB)], 0.0, None, ALU.add)
                V.tensor_scalar(x1b[:, :, E0], ixf[:, :, 0], 0.0, None, ALU.add)
                step.link(V.tensor_scalar(eden[:], edif[:], 1.0, None, ALU.add))
                step.link(V.reciprocal(wt0[:], eden[:]))
                step.link(V.tensor_tensor(x1b[:, :, W1], wt0[:], edif[:], ALU.mult))
                step.link(V.tensor_tensor(x1b[:, :, DW], wt0[:], x1b[:, :, W1], ALU.subtract))

            def place(b):
                dve.wait_ge(mask_ready, b)
                step.link(V.tensor_reduce(new8[:], mask[:].rearrange("p j e -> p e j"), AX.X, ALU.add))
                dve.wait_ge(rank_made, b)
                V.tensor_tensor(cum[:], cum[:], new8[:], ALU.add).then_inc(cum_ready, 1)
                step.link(V.tensor_tensor(rank8[:], psL.rearrange("p (j e) -> p j e", e=E),
                                          base8[:].unsqueeze(1).to_broadcast([P, TB, E]), ALU.add))
                both_k = oh[:].rearrange("p (j k) e -> p j k e", k=TOP)
                picks = pick[:].rearrange("p (j k) e -> p j k e", k=TOP)
                for k in range(TOP):
                    last = V.tensor_tensor(picks[:, :, k, :], both_k[:, :, k, :], rank8[:], ALU.mult)
                step.link(last)
                step.link(V.tensor_reduce(slotf[:], pick[:], AX.X, ALU.add))
                V.tensor_copy(idx_now[:], slotf[:]).then_inc(idx_ready, 1)

            def shared_product(u):
                dve.wait_ge(tanh_done, u + 1)
                dve.wait_ge(G_made, u + 1)
                V.scalar_tensor_tensor(sg[:], sg[:], 1.0, psG[:], ALU.add, ALU.mult).then_inc(silu_done, 1)
                dve.wait_ge(silu_done, u + 1)
                dve.wait_ge(U_made, u + 1)
                if not isinstance(u, int) or u > 0:
                    dve.wait_ge(H_turned, u)
                V.scalar_tensor_tensor(hp[:], sg[:], 0.5, psU[:], ALU.mult, ALU.mult).then_inc(hp_ready, 1)

            def add_shared(u, b):
                dve.wait_ge(O_made, u + 1)
                dve.wait_ge(x1_kept, b)
                row = total[:, ds(u, 1), :].rearrange("p o d -> p (o d)")
                V.tensor_tensor(row, row, psM[:, 0:D], ALU.add).then_inc(add_done, 1)

            def shared_step(b, m, second):
                if m == STATS:
                    dve.wait_ge(v_kept, b)
                    alone(dve)
                    stats([x1b[:, j, 0:D] for j in range(TB)])
                if m == NORM:
                    norm(b)
                if m == CHOOSE:
                    choose(b)
                if m == WEIGH:
                    weigh(b)
                if m == PLACE:
                    place(b)
                for u, j, of in tiles_at(b, m, ADD, second):
                    add_shared(u, of)

            SCAN = 19

            def scan_batch(b, g0, first, last, second=False):
                for n in range(N):
                    if not first:
                        for u, j, _ in tiles_at(b, n, PRODUCT, second):
                            shared_product(u)
                    if n not in BY_POOL:
                        inject(dve, b, g0, n, first)
                    if n >= 1:
                        project(g0 + (n - 1), n - 1, first)
                    elif not first:
                        project(g0 - 1, N - 1, False)
                    scan(b, g0 + n, n, first)
                    if first and n == 9:
                        finish_delta(NB - 1)
                    if not first:
                        shared_step(b, n, second)
                if last:
                    project(g0 + (N - 1), N - 1, False)

            step.start(NB * PREP)
            scan_batch(0, 0, True, False)
            dve.wait_ge(du_ready, NB)
            scan_batch(1, N, False, False, True)
            with dve.Fori(2, NB - 1) as b:
                step.start(b * SCAN + (NB * PREP - SCAN))
                scan_batch(b, b * N, False, False)
            step.start((NB - 2) * SCAN + NB * PREP)
            scan_batch(NB - 1, (NB - 1) * N, False, True)
            left = NT - TB - 2
            if not done_in_scan(PRODUCT):
                shared_product(left)
            dve.wait_ge(v_kept, NB)
            alone(dve)
            stats([x1b[:, j, 0:D] for j in range(TB)])
            add_shared(left, NB - 1)
            shared_product(left + 1)
            norm(NB)
            add_shared(left + 1, NB - 1)
            choose(NB)
            weigh(NB)
            place(NB)
            shared_product(NT - TB)
            dve.wait_ge(count_made, 1)
            step.link(V.tensor_copy(cnt[:], psN))
            V.tensor_copy(cnti[:], cnt[:]).then_inc(counted, 1)
            step.link(V.tensor_scalar(pgi[:], cnt[:], float(P - 1), None, ALU.add))
            step.link(V.tensor_single_scalar(pgs[:], pgi[:], P.bit_length() - 1, ALU.arith_shift_right))
            step.link(V.tensor_copy(pages[:], pgs[:]))
            step.link(V.tensor_tensor_scan(ends[:], onerow[:], pages[:], 0.0, ALU.mult, ALU.add))
            step.link(V.tensor_scalar(skip[:], pages[:], -float(P), float(REGION), ALU.mult, ALU.add))
            step.link(V.tensor_tensor(past, jrow[:].unsqueeze(2).to_broadcast([P, RT, E]),
                                      ends[:].unsqueeze(1).to_broadcast([P, RT, E]), ALU.is_ge))
            step.link(V.tensor_tensor(jump, past[0:1], skip[0:1, :].unsqueeze(1).to_broadcast([1, RT, E]), ALU.mult))
            step.link(V.tensor_reduce(esum[:], past, AX.X, ALU.add))
            step.link(V.tensor_reduce(rsum[:], jump, AX.X, ALU.add))
            step.link(V.tensor_tensor(rowf[:], rsum[:], jbase[:], ALU.add))
            step.link(V.tensor_copy(tab_r[:], rowf[:]))
            V.tensor_scalar(tab_e[:], esum[0:1, :], float(E - 1), None, ALU.min).then_inc(table_ready, 1)

            for j in range(1, TB):
                shared_product(NT - TB + j)
                add_shared(NT - TB + j - 1, NB)
            add_shared(NT - 1, NB)

            def read_meta(j, s, fills):
                dve.wait_ge(slot_in[s], fills * 16)
                if not isinstance(j, int) or j >= PAGES:
                    dve.wait_ge(added, (j - (PAGES - 1)) * 16)
                alone(dve)
                here = page_in[:, s, :]
                V.tensor_copy(row_page[:, s:s + 1], here[:, ID:ID + 1])
                step.link(V.tensor_scalar(w_match[:, s:s + 1], here[:, E0:E0 + 1], esum[:, ds(j, 1)],
                                          here[:, DW:DW + 1], ALU.is_equal, ALU.mult))
                V.tensor_tensor(w_page[:, s:s + 1], w_match[:, s:s + 1], here[:, W1:W1 + 1],
                                ALU.add).then_inc(meta_read, 1)

            def keep_y(j, s):
                dve.wait_ge(O_made, j + (NT + 1))
                dve.wait_ge(meta_read, j + 1)
                if not isinstance(j, int) or j > 1:
                    dve.wait_ge(added, (j - 1) * 16)
                V.tensor_scalar(yo[:, s % 2, :], psO[:, 0:D], w_page[:, s % PAGES:s % PAGES + 1], None,
                                ALU.mult).then_inc(y_read, 1)

            def routed_tile(j, s, fills):
                read_meta(j, s, fills)
                dve.wait_ge(silu_done, j + (NT + 1))
                dve.wait_ge(U_made, j + (NT + 1))
                dve.wait_ge(H_turned, j + NT)
                V.tensor_tensor(hp[:], sg[:], psU[:], ALU.mult).then_inc(hp_ready, 1)
                if not isinstance(j, int) or j > 0:
                    keep_y(j - 1, s - 1)

            for j in range(PAGES):
                routed_tile(j, j, 1)
            paged = step.n + step.base
            with dve.Fori(1, LOOPED) as i:
                step.start(i * PAGES + (paged - PAGES))
                for s in range(PAGES):
                    routed_tile(i * PAGES + s, s, i + 1)
            step.start(paged + (LOOPED - 1) * PAGES)
            for j in range(LOOPED * PAGES, RT):
                routed_tile(j, j % PAGES, j // PAGES + 1)
            keep_y(RT - 1, RT - 1)

            step.start(paged + RT - PAGES)
            for half in range(2):
                a, z = half * HT, half * HT + HT
                for t in range(a, z):
                    if t % TB == 0:
                        dve.wait_ge(final_in[t // TB], 16)
                    last = V.bn_stats(st6_fin[:, t, :], vfin[:, t, :])
                step.link(last)
                for t in range(a, z):
                    last = V.bn_aggr(mv_fin[:, t, :], st6_fin[:, t, :])
                step.link(last)
                V.tensor_scalar(ve_fin[:, a:z], mv_fin[:, a:z, 1], EPS, None, ALU.add).then_inc(ve_ready, 1)
            for half in range(2):
                a, z = half * HT, half * HT + HT
                dve.wait_ge(root_ready, half + 1)
                step.link(V.tensor_tensor(sq_fin[:, a:z], r0_fin[:, a:z], r0_fin[:, a:z], ALU.mult))
                step.link(V.tensor_tensor(vr_fin[:, a:z], sq_fin[:, a:z], ve_fin[:, a:z], ALU.mult))
                step.link(V.tensor_scalar(r3_fin[:, a:z], vr_fin[:, a:z], -0.5, 1.5, ALU.mult, ALU.add))
                step.link(V.tensor_tensor(rstd_fin[:, a:z], r0_fin[:, a:z], r3_fin[:, a:z], ALU.mult))
                V.scalar_tensor_tensor(shift_fin[:, a:z], mv_fin[:, a:z, 0], -1.0, rstd_fin[:, a:z],
                                       ALU.mult, ALU.mult).then_inc(scale_ready, 1)
                for t in range(a + BY_ACT, z):
                    last = V.tensor_scalar(vfin[:, t, :], vfin[:, t, :], mv_fin[:, t, 0:1], rstd_fin[:, t:t + 1],
                                           ALU.subtract, ALU.mult)
                last.then_inc(out_ready, 1)


_INS = ["L0_attn_x", "L0_attn_A_log", "L0_attn_D", "L0_attn_x_proj_w", "L0_attn_dt_proj_w", "L0_attn_dt_proj_b",
        "L0_ffn_gate_w", "L0_ffn_w_gate_up", "L0_ffn_w_down", "L0_ffn_shared_gate_up", "L0_ffn_shared_down"]


def kernel(**inputs):
    import numpy as _np
    import concourse.bacc as _bacc
    from concourse import mybir as _mybir
    from concourse.bass_utils import run_bass_kernel_spmd as _run

    nc = _bacc.Bacc("TRN2", target_bir_lowering=False, num_devices=1)
    arrays, args = {}, []
    for name in _INS:
        a = _np.ascontiguousarray(inputs[name])
        arrays[f"in_{name}"] = a
        args.append(nc.dram_tensor(f"in_{name}", a.shape, _mybir.dt.from_np(a.dtype), kind="ExternalInput").ap())
    out = nc.dram_tensor("out_0", inputs["L0_attn_x"].shape, _mybir.dt.float32, kind="ExternalOutput").ap()
    mamba_moe(nc, *args, out)
    r = _run(nc, [arrays], core_ids=[0])
    return r.results[0]["out_0"]
```
